# Optimizing a Trainium2 kernel written in Bass

```python
import numpy as np
import jax
import jax.numpy as jnp

def _softmax(x, axis=-1):
    return jax.nn.softmax(x, axis=axis)

def _gelu(x):
    return jax.nn.gelu(x, approximate=True)

def _silu(x):
    return jax.nn.silu(x)

def _sigmoid(x):
    return jax.nn.sigmoid(x)

def _layernorm(x, axis=-1, eps=1e-05):
    m = jnp.mean(x, axis=axis, keepdims=True)
    v = jnp.var(x, axis=axis, keepdims=True)
    return (x - m) / jnp.sqrt(v + eps)

def _scatter_add(tgt, idx, src, axis=0):
    return tgt.at[idx].add(src)

def _segment_sum(src, seg, n):
    return jax.ops.segment_sum(src, seg, n)
kernel_name = 'mk_adaln_ffn_d1_seqx_r4_9eb8d8'

def setup_inputs(seed: int=0):
    np.random.seed(seed)
    _w = jnp.asarray

    def _rec_inputs():
        import jax
        import jax.numpy as jnp
        _rk = jax.random.key(seed)
        x = -7.109e-05 + 0.9999 * jax.random.normal(jax.random.fold_in(_rk, 1), (4, 512, 512), jnp.float32)
        _lenS = 512 - jax.random.randint(jax.random.fold_in(_rk, 7), (4,), 0, max(1, 512 // 4) + 1, jnp.int32)
        _lenS2 = 512 - jax.random.randint(jax.random.fold_in(_rk, 8), (4,), 0, max(1, 512 // 4) + 1, jnp.int32)
        itok_B_0_6 = jax.random.randint(jax.random.fold_in(_rk, 11), (4,), 0, 7, jnp.int32)
        return (x, itok_B_0_6)
    x, itok_B_0_6 = _rec_inputs()

    def _L0_cond_setup():
        import jax, jax.numpy as jnp
        import numpy as np
        B, T, D_IN, D_OUT = (16, 512, 512, 512)
        N_ADAPTERS, RANK = (8, 16)
        key = jax.random.key(seed)
        k_x, k_w, k_a, k_b, k_s, k_idx = jax.random.split(key, 6)
        x = jax.random.normal(k_x, (B, T, D_IN), dtype=jnp.float32)
        W = jax.random.normal(k_w, (D_OUT, D_IN), dtype=jnp.float32) * (1.0 / np.sqrt(D_IN))
        A = jax.random.normal(k_a, (N_ADAPTERS, RANK, D_IN), dtype=jnp.float32) * 0.02
        Bm = jax.random.normal(k_b, (N_ADAPTERS, D_OUT, RANK), dtype=jnp.float32) * 0.02
        scalings = jnp.ones((N_ADAPTERS,), dtype=jnp.float32)
        adapter_idx = jax.random.randint(k_idx, (B,), 0, N_ADAPTERS, dtype=jnp.int32)
        return {'x': x, 'W': W, 'A': A, 'Bm': Bm, 'scalings': scalings, 'adapter_idx': adapter_idx}
    _L0_cond_all = _L0_cond_setup()
    _L0_cond_in = {k: v for k, v in _L0_cond_all.items() if k in ('W', 'A', 'Bm', 'scalings')}
    del _L0_cond_all

    def _L0_ffn_setup():
        import jax, jax.numpy as jnp
        import numpy as np
        import math
        B, S, D = (2, 512, 512)
        P = 4
        PW = 2
        L = 2
        STD = 0.02
        EPS = 1e-05

        def _layer_norm(x, g, b):
            m = jnp.mean(x, axis=-1, keepdims=True)
            v = jnp.mean(jnp.square(x - m), axis=-1, keepdims=True)
            return (x - m) * jax.lax.rsqrt(v + EPS) * g + b
        key = jax.random.key(seed)
        ks = jax.random.split(key, 16)
        n = lambda k, shape: jax.random.normal(k, shape, dtype=jnp.float32) * STD
        inp = {'x': jax.random.normal(ks[0], (B, S, D), dtype=jnp.float32), 'amp_w': n(ks[1], (D, D)), 'amp_b': jnp.zeros((D,), jnp.float32), 'ph_w': n(ks[2], (D, D)), 'ph_b': jnp.zeros((D,), jnp.float32), 'ent_w': n(ks[3], (L, D, P * D)), 'ent_b': jnp.zeros((L, P * D), jnp.float32), 'ent_pw': n(ks[4], (L, P * D, D)), 'ent_pb': jnp.zeros((L, D), jnp.float32), 'path_w': n(ks[5], (L, PW, D, D)), 'path_b': jnp.zeros((L, PW, D), jnp.float32), 'phase': jax.random.normal(ks[6], (L, PW, D), dtype=jnp.float32), 'ln3_g': jnp.ones((L, D), jnp.float32), 'ln3_b': jnp.zeros((L, D), jnp.float32), 'ln4_g': jnp.ones((L, D), jnp.float32), 'ln4_b': jnp.zeros((L, D), jnp.float32)}
        return inp
    _L0_ffn_all = _L0_ffn_setup()
    _L0_ffn_in = {k: v for k, v in _L0_ffn_all.items() if k in ('amp_w', 'amp_b', 'ph_w', 'ph_b', 'ent_w', 'ent_b', 'ent_pw', 'ent_pb', 'path_w', 'path_b', 'phase', 'ln3_g', 'ln3_b', 'ln4_g', 'ln4_b')}
    del _L0_ffn_all
    return {'x': x, 'itok_B_0_6': itok_B_0_6, 'L0_cond_W': _L0_cond_in['W'], 'L0_cond_A': _L0_cond_in['A'], 'L0_cond_Bm': _L0_cond_in['Bm'], 'L0_cond_scalings': _L0_cond_in['scalings'], 'L0_ffn_amp_w': _L0_ffn_in['amp_w'], 'L0_ffn_amp_b': _L0_ffn_in['amp_b'], 'L0_ffn_ph_w': _L0_ffn_in['ph_w'], 'L0_ffn_ph_b': _L0_ffn_in['ph_b'], 'L0_ffn_ent_w': _L0_ffn_in['ent_w'], 'L0_ffn_ent_b': _L0_ffn_in['ent_b'], 'L0_ffn_ent_pw': _L0_ffn_in['ent_pw'], 'L0_ffn_ent_pb': _L0_ffn_in['ent_pb'], 'L0_ffn_path_w': _L0_ffn_in['path_w'], 'L0_ffn_path_b': _L0_ffn_in['path_b'], 'L0_ffn_phase': _L0_ffn_in['phase'], 'L0_ffn_ln3_g': _L0_ffn_in['ln3_g'], 'L0_ffn_ln3_b': _L0_ffn_in['ln3_b'], 'L0_ffn_ln4_g': _L0_ffn_in['ln4_g'], 'L0_ffn_ln4_b': _L0_ffn_in['ln4_b']}

def reference(x, itok_B_0_6, L0_cond_W, L0_cond_A, L0_cond_Bm, L0_cond_scalings, L0_ffn_amp_w, L0_ffn_amp_b, L0_ffn_ph_w, L0_ffn_ph_b, L0_ffn_ent_w, L0_ffn_ent_b, L0_ffn_ent_pw, L0_ffn_ent_pb, L0_ffn_path_w, L0_ffn_path_b, L0_ffn_phase, L0_ffn_ln3_g, L0_ffn_ln3_b, L0_ffn_ln4_g, L0_ffn_ln4_b):
    import jax
    import jax.numpy as jnp

    def _L0_cond_ref(x, W, A, Bm, scalings, adapter_idx):
        import jax, jax.numpy as jnp
        import numpy as np
        B, T, D_IN, D_OUT = (16, 512, 512, 512)
        N_ADAPTERS, RANK = (8, 16)
        H = jnp.einsum('btd,od->bto', x, W)
        A_b = A[adapter_idx]
        B_b = Bm[adapter_idx]
        s_b = scalings[adapter_idx]
        xa = jnp.einsum('btd,brd->btr', x, A_b)
        delta = jnp.einsum('btr,bor->bto', xa, B_b)
        delta = jax.lax.stop_gradient(delta * s_b[:, None, None])
        return H + delta

    def _L0_ffn_ref(x, amp_w, amp_b, ph_w, ph_b, ent_w, ent_b, ent_pw, ent_pb, path_w, path_b, phase, ln3_g, ln3_b, ln4_g, ln4_b):
        import jax, jax.numpy as jnp
        import numpy as np
        import math
        B, S, D = (2, 512, 512)
        P = 4
        PW = 2
        L = 2
        STD = 0.02
        EPS = 1e-05

        def _layer_norm(x, g, b):
            m = jnp.mean(x, axis=-1, keepdims=True)
            v = jnp.mean(jnp.square(x - m), axis=-1, keepdims=True)
            return (x - m) * jax.lax.rsqrt(v + EPS) * g + b
        amp = jax.nn.sigmoid(x @ amp_w + amp_b)
        ph = jnp.tanh(x @ ph_w + ph_b) * math.pi
        h = (jnp.cos(ph) + jnp.sin(ph)) * amp
        for l in range(L):
            e = h @ ent_w[l] + ent_b[l]
            ent = e @ ent_pw[l] + ent_pb[l]
            h = _layer_norm(h + ent, ln3_g[l], ln3_b[l])
            t = jnp.einsum('bsd,pdf->pbsf', h, path_w[l]) + path_b[l][:, None, None, :]
            mod = jnp.cos(phase[l]) + jnp.sin(phase[l])
            interf = jnp.sum(t * mod[:, None, None, :], axis=0)
            h = _layer_norm(h + interf, ln4_g[l], ln4_b[l])
        return h
    x = x + _L0_ffn_ref(_L0_cond_ref(x, L0_cond_W, L0_cond_A, L0_cond_Bm, L0_cond_scalings, itok_B_0_6), L0_ffn_amp_w, L0_ffn_amp_b, L0_ffn_ph_w, L0_ffn_ph_b, L0_ffn_ent_w, L0_ffn_ent_b, L0_ffn_ent_pw, L0_ffn_ent_pb, L0_ffn_path_w, L0_ffn_path_b, L0_ffn_phase, L0_ffn_ln3_g, L0_ffn_ln3_b, L0_ffn_ln4_g, L0_ffn_ln4_b)
    return x

_drawn_inputs = setup_inputs


def setup_inputs(seed=0):
    import zlib

    import numpy as np

    out = dict(_drawn_inputs(seed))
    spreads = {'L0_cond_scalings': (1.0, 0.6),
     'L0_ffn_amp_b': (0.0, 0.27),
     'L0_ffn_ph_b': (0.0, 0.1),
     'L0_ffn_ent_b': (0.0, 0.1),
     'L0_ffn_ent_pb': (0.0, 0.1),
     'L0_ffn_path_b': (0.0, 0.1),
     'L0_ffn_ln3_g': (1.0, 0.2),
     'L0_ffn_ln3_b': (0.0, 0.1),
     'L0_ffn_ln4_g': (1.0, 0.2),
     'L0_ffn_ln4_b': (0.0, 0.1)}
    factors = {}
    for name, (base, spread) in spreads.items():
        noise = np.random.default_rng([zlib.crc32(name.encode()), seed]).standard_normal(out[name].shape)
        drawn = base * np.exp(spread * noise) if base else spread * noise
        out[name] = jnp.asarray(drawn.astype(out[name].dtype))
    for name, factor in factors.items():
        out[name] = (out[name] * factor).astype(out[name].dtype)
    return out
```

```python
import concourse.bass as bass
from concourse import mybir
from contextlib import ExitStack
import math

F32 = mybir.dt.float32
F32R = mybir.dt.float32r
I32 = mybir.dt.int32
ACT = mybir.ActivationFunctionType
ALU = mybir.AluOpType

P = 128
D = 512
B = 4
T = 512
KT = D // P
NT = T // P
L = 2
F = 2048
FT = F // P
NADAPT, RANK = 8, 16
EPS = 1e-5
STAGES = 2 * L
RING = 4
NSLICE = 8

AMP_B, PH_B = 0, KT
ENT_B = 2 * KT
LN3_G = ENT_B + L * FT
LN3_B = LN3_G + L * KT
LN4_G = LN3_B + L * KT
LN4_B = LN4_G + L * KT
SCALE = LN4_B + L * KT
NCOLS = SCALE + 1


ROUND = 1.5 * 2 ** 23
TWO_PI = [6.28125, round((2 * math.pi - 6.28125) * 2 ** 20) / 2 ** 20]
TWO_PI.append(2 * math.pi - sum(TWO_PI))
PI_BELOW = 3.1415925


class Tally:

    def __init__(self, sem):
        self.sem, self.count, self.loop = sem, 0, 0

    def enter(self, loop):
        self.loop, self.start = loop, self.count

    def leave(self, iterations):
        self.loop, self.count = 0, self.start + iterations * (self.count - self.start)

    def inc(self, instruction, engine=None):
        self.count += 1
        instruction.then_inc(self.sem, 1)
        if engine is not None:
            engine.wait_ge(self.sem, self.loop + self.count)


def build(nc, xt, xr, wc, ap, bt, aa, idx, cols, phase, pathb, entpb, gb_rows, ent, path, out):
    ctx = ExitStack()
    with ctx:
        def sb(name, shape, dt=F32):
            return ctx.enter_context(nc.sbuf_tensor(name, shape, dt))

        def sem(name):
            return ctx.enter_context(nc.semaphore(name))

        stage_h = sb("stage_h", [P, STAGES, KT, D], F32R)
        stage_l = sb("stage_l", [P, STAGES, KT, D], F32R)
        fold = sb("fold", [P, KT, 2 * D])
        q_h = sb("q_h", [P, 2 * D], F32R)
        q_l = sb("q_l", [P, 2 * D], F32R)
        bias = sb("bias", [P, STAGES, D])
        gb = sb("gb", [P, 2, D])
        a_all = sb("a_all", [P, D])
        col = sb("col", [P, NCOLS])
        ident = sb("ident", [P, P])
        ones = sb("ones", [P, P])
        mb_h = sb("mb_h", [P, KT, 2 * D], F32R)
        mb_l = sb("mb_l", [P, KT, 2 * D], F32R)
        x_h = sb("x_h", [P, KT, T], F32R)
        x_l = sb("x_l", [P, KT, T], F32R)
        am_h = sb("am_h", [P, D], F32R)
        am_l = sb("am_l", [P, D], F32R)
        h_h = sb("h_h", [P, KT, T], F32R)
        h_l = sb("h_l", [P, KT, T], F32R)
        z_h = sb("z_h", [P, KT, T], F32R)
        z_l = sb("z_l", [P, KT, T], F32R)
        amp = sb("amp", [P, KT, T])
        work = sb("work", [P, NT, D])
        mod = sb("mod", [P, 2, D])
        raw = sb("raw", [P, 3, 2 * D])
        junk = sb("junk", [P, D])
        idx_i = sb("idx_i", [P, B], I32)
        idx_f = sb("idx_f", [P, B])
        pcol_i = sb("pcol_i", [P, 1], I32)
        pcol = sb("pcol", [P, 1])
        pick = sb("pick", [P, B])
        tmp4 = sb("tmp4", [P, B])
        rowsum = sb("rowsum", [P, 16 + STAGES])
        negmean = sb("negmean", [P, 16 + STAGES])
        layer_rows = sb("layer_rows", [P, L])
        half_pi = sb("half_pi", [P, 1])
        minus_quarter = sb("minus_quarter", [P, 1])
        sumsq = sb("sumsq", [P, 16])
        var = sb("var", [P, 16])
        minus_half = sb("minus_half", [P, 1])
        eps_sum = sb("eps_sum", [P, 1])
        newton_a = sb("newton_a", [P, 1])
        newton_b = sb("newton_b", [P, 1])
        root = sb("root", [P, 16])
        corr = sb("corr", [P, 16])
        rstd = sb("rstd", [P, 16])

        bank = [ctx.enter_context(nc.psum_tensor(f"bank{i}", [P, 512], F32)) for i in range(8)]

        raw_slot = [raw[:, 0, :], raw[:, 1, :], raw[:, 2, :],
                    work[:, 0:2, :].rearrange("p a b -> p (a b)")]
        ring_h = [h_h[:, 0:2, :], h_h[:, 2:4, :], z_h[:, 0:2, :], z_h[:, 2:4, :]]
        ring_l = [h_l[:, 0:2, :], h_l[:, 2:4, :], z_l[:, 0:2, :], z_l[:, 2:4, :]]
        tile = [work[:, 2, :], work[:, 3, :]]
        b_raw = work[:, 2, :]
        res = raw[:, 0:2, :].rearrange("p a (b c) -> p (a b) c", b=2)
        lsum = [raw[:, 2, 0:D], raw[:, 2, D:2 * D]]
        lsum_first = tile
        mod_rows = junk[0:4, :]

        fold_in = [sem(f"fold_in{k}") for k in range(KT)]
        small_in = sem("small_in")
        rows_in = sem("rows_in")
        entpb_in = sem("entpb_in")
        b_in = sem("b_in")
        a_in = sem("a_in")
        gb_in = sem("gb_in")
        raw_in = [sem(f"raw_in{s}") for s in range(RING)]
        x_in = sem("x_in")
        res_in = sem("res_in")
        stored = [sem(f"stored{i}") for i in range(NT)]
        const_done = sem("const_done")
        pool_chain = sem("pool_chain")
        dve_chain = sem("dve_chain")
        act_chain = sem("act_chain")
        reduced = sem("reduced")
        trig = sem("trig")
        rows_done = sem("rows_done")
        hi_done = sem("hi_done")
        lo_done = sem("lo_done")
        step_done = sem("step_done")
        acc_done = sem("acc_done")
        b_hi = sem("b_hi")
        b_lo = sem("b_lo")
        m_act = sem("m_act")
        m_dve = sem("m_dve")
        q_mm = sem("q_mm")
        q_hi = sem("q_hi")
        q_lo = sem("q_lo")
        mod_mm = sem("mod_mm")
        mod_in = sem("mod_in")
        scaled = sem("scaled")
        summed = sem("summed")
        centred = sem("centred")
        stage_hi = sem("stage_hi")
        stage_done = sem("stage_done")
        bias_mm = sem("bias_mm")
        bias_sum = sem("bias_sum")
        y_mm = sem("y_mm")
        s_mm = sem("s_mm")
        l_mm = sem("l_mm")
        t_mm = sem("t_mm")
        v_done = sem("v_done")
        sq_done = sem("sq_done")
        r_done = sem("r_done")
        zhi = sem("zhi")
        zlo = sem("zlo")
        lsum_done = sem("lsum_done")
        lhi = sem("lhi")
        llo = sem("llo")
        xhi = sem("xhi")
        xlo = sem("xlo")
        s_act = sem("s_act")
        abs_done = sem("abs_done")
        sin_done = sem("sin_done")
        h_done = sem("h_done")
        hhi = sem("hhi")
        hlo = sem("hlo")
        res_done = sem("res_done")
        out_done = sem("out_done")

        STEPS = ([("E", 0, k) for k in range(4)] + [("P", 0, k) for k in range(4)]
                 + [("E", 0, k) for k in range(4, FT)] + [("P", 1, k) for k in range(4)]
                 + [("E", 1, k) for k in range(FT)])
        at = {step: g for g, step in enumerate(STEPS)}

        def raw_value(g):
            return 16 * (g // RING + 1)

        def fold_bank(l, m):
            return 4 * (1 - l) + m

        def gain_col(st, k):
            if st == 0:
                return None
            base = LN3_G + (st // 2) * KT if st % 2 else LN4_G
            return col[:, base + k:base + k + 1]

        def shift_col(st, k):
            if st == 0:
                return None
            base = LN3_B + (st // 2) * KT if st % 2 else LN4_B
            return col[:, base + k:base + k + 1]

        PATH_U = [l * KT for l in range(L)]
        ENT_U = [(L + l) * KT for l in range(L)]
        ITEMS = NSLICE + 1

        def order(with_next):
            y = [("Y", st, i) for st in range(STAGES) for i in range(NT)]
            s = [("S", s, 0) for s in range(NSLICE)] if with_next else []
            return y[:12] + s + y[12:]

        LAG = 2
        LORA_AT = 2
        X_AT = (10, 11)

        def transposed(item):
            return item[0] == "Y" and item[1] < STAGES - 1

        block = ctx.enter_context(nc.Block())

        @block.sync
        def _(sp):
            for k in range(KT):
                sp.dma_start(amp[:, k, :], wc[k]).then_inc(fold_in[k], 16)
                sp.dma_start(fold[:, k, :], ap[k]).then_inc(fold_in[k], 16)
            sp.dma_start(b_raw, bt).then_inc(b_in, 16)
            sp.dma_start(a_all[:, :], aa).then_inc(a_in, 16)
            for g, (kind, l, k) in enumerate(STEPS):
                if g == RING - 1:
                    sp.wait_ge(rows_done, L + 1)
                if g >= RING:
                    was, wl, wk = STEPS[g - RING]
                    if was == "E":
                        sp.wait_ge(acc_done, wl * FT + wk + 2)
                    else:
                        sp.wait_ge(scaled, wl * KT + wk + 1)
                sp.dma_start(raw_slot[g % RING], (ent if kind == "E" else path)[l, k]).then_inc(
                    raw_in[g % RING], 16)
                if g == 1:
                    sp.wait_ge(const_done, 2)
                    for layer in range(L):
                        sp.dma_start(bias[0:1, 2 * layer, :], entpb[layer:layer + 1, :]).then_inc(entpb_in, 16)
                if g == RING:
                    sp.wait_ge(lo_done, KT)
                    sp.dma_start(amp[:, :, :], xt[0]).then_inc(x_in, 16)
                    sp.dma_start(gb[:, :, :], gb_rows.partition_broadcast(P)).then_inc(gb_in, 16)

            def batch(b, with_next):
                if with_next:
                    sp.wait_ge(h_done, b * KT + KT)
                    sp.dma_start(amp[:, :, :], xt[bass.ds(b + 1, 1)].rearrange(
                        "a p k t -> (a p) k t")).then_inc(x_in, 16)
                for i in range(NT):
                    sp.wait_ge(out_done, b * NT + i + 1)
                    sp.dma_start(out[bass.ds(b, 1)].rearrange("a p t d -> (a p) t d")[:, i, :],
                                 res[:, i, :]).then_inc(stored[i], 16)
                if with_next:
                    for i in range(NT):
                        sp.wait_ge(stored[i], b * 16 + 16)
                    sp.dma_start(res, xr[bass.ds(b + 1, 1)].rearrange(
                        "a p t d -> (a p) t d")).then_inc(res_in, 16)

            sp.wait_ge(acc_done, L * FT + 1)
            sp.dma_start(res, xr[0]).then_inc(res_in, 16)
            with sp.Fori(0, B - 1) as b:
                batch(b, True)
            batch(B - 1, False)
            for i in range(NT):
                sp.wait_ge(stored[i], B * 16)

        @block.gpsimd
        def _(pool):
            own = Tally(pool_chain)
            own.inc(nc.gpsimd.memset(ident[:, :], 0.0), pool)
            nc.gpsimd.affine_select(out=ident[:, :], in_=ident[:, :], compare_op=ALU.not_equal, fill=1.0,
                                    base=0, pattern=[[-1, P]], channel_multiplier=1).then_inc(const_done, 1)
            nc.gpsimd.memset(bias[:, :, :], 0.0).then_inc(const_done, 1)
            nc.gpsimd.memset(half_pi[:, :], math.pi / 2).then_inc(const_done, 1)
            own.inc(nc.gpsimd.memset(minus_quarter[:, :], -0.25), pool)
            nc.gpsimd.iota(pcol_i[:, :], [[0, 1]], base=0, channel_multiplier=1).then_inc(const_done, 1)
            nc.gpsimd.memset(ones[:, :], 1.0).then_inc(const_done, 1)
            own.inc(nc.gpsimd.memset(minus_half[:, :], -0.5), pool)
            own.inc(nc.gpsimd.memset(eps_sum[:, :], D * EPS), pool)
            own.inc(nc.gpsimd.memset(newton_a[:, :], -0.5 * math.sqrt(D)), pool)
            own.inc(nc.gpsimd.memset(newton_b[:, :], 1.5 * math.sqrt(D)), pool)

            for l in range(L):
                pool.wait_ge(mod_in, 2 * (l + 1))
                for k in range(KT):
                    u = PATH_U[l] + k
                    g = at["P", l, k]
                    slot = raw_slot[g % RING].rearrange("p (a b) -> p a b", a=2)
                    pool.wait_ge(raw_in[g % RING], raw_value(g))
                    own.inc(nc.gpsimd.tensor_tensor(slot, slot, mod[:, :, :], ALU.mult), pool)
                    if u >= 2:
                        pool.wait_ge(stage_done, u - 1)
                    elif u == 0:
                        pool.wait_ge(b_lo, 1)
                    if u == PATH_U[1]:
                        pool.wait_ge(llo, ITEMS)
                    nc.gpsimd.tensor_tensor(tile[u % 2], slot[:, 0, :], slot[:, 1, :],
                                            ALU.add).then_inc(scaled, 1)

            def token_scale(n, st, i):
                c = slice(st * NT + i, st * NT + i + 1)
                pool.wait_ge(sq_done, n + 1)
                own.inc(nc.gpsimd.tensor_tensor(var[:, c], sumsq[:, c], eps_sum[:, :], ALU.add), pool)
                own.inc(nc.gpsimd.tensor_tensor(root[:, c], var[:, c], minus_half[:, :], ALU.pow), pool)
                own.inc(nc.gpsimd.tensor_tensor(corr[:, c], root[:, c], root[:, c], ALU.mult), pool)
                own.inc(nc.gpsimd.tensor_tensor(corr[:, c], corr[:, c], var[:, c], ALU.mult), pool)
                own.inc(nc.gpsimd.tensor_tensor(corr[:, c], corr[:, c], newton_a[:, :], ALU.mult), pool)
                own.inc(nc.gpsimd.tensor_tensor(corr[:, c], corr[:, c], newton_b[:, :], ALU.add), pool)
                nc.gpsimd.tensor_tensor(rstd[:, c], root[:, c], corr[:, c], ALU.mult).then_inc(r_done, 1)

            pool.wait_ge(gb_in, 16)
            links = 6 * STAGES * NT
            with pool.Fori(0, B) as b:
                own.enter(b * links)
                for st in range(STAGES):
                    for i in range(NT):
                        token_scale(b * 16 + st * NT + i, st, i)
                    if st == 0:
                        pool.wait_ge(res_in, b * 16 + 16)
                        for i in range(NT):
                            nc.gpsimd.tensor_tensor(res[:, i, :], res[:, i, :], gb[:, 1, :],
                                                    ALU.add).then_inc(res_done, 1)
            own.leave(B)

        @block.scalar
        def _(act):
            act.dma_start(gb[0:4, 0, :], phase).then_inc(rows_in, 16)
            act.dma_start(gb[0:4, 1, :], pathb).then_inc(rows_in, 16)
            act.dma_start(col[:, :], cols).then_inc(small_in, 16)
            act.dma_start(idx_i[:, :], idx.partition_broadcast(P)).then_inc(small_in, 16)

            act.wait_ge(reduced, 1)
            nc.scalar.activation(work[0:4, 1, :], gb[0:4, 0, :], ACT.Sin).then_inc(trig, 1)
            nc.scalar.activation(work[0:4, 0, :], gb[0:4, 0, :], ACT.Abs).then_inc(act_chain, 1)
            act.wait_ge(act_chain, 1)
            act.wait_ge(const_done, 3)
            nc.scalar.activation(work[0:4, 0, :], work[0:4, 0, :], ACT.Sin, scale=-1.0,
                                 bias=half_pi[0:4, :]).then_inc(trig, 1)

            for k in range(KT):
                act.wait_ge(fold_in[k], 32)
                nc.scalar.activation(x_h[:, k, :], amp[:, k, :], ACT.Copy)
                nc.scalar.activation(mb_h[:, k, :], fold[:, k, :], ACT.Copy).then_inc(hi_done, 1)
            act.wait_ge(b_in, 16)
            nc.scalar.activation(am_h[:, :], b_raw, ACT.Copy).then_inc(b_hi, 1)

            def ent_high(slot, e, landed):
                act.wait_ge(raw_in[slot], landed)
                act.wait_ge(step_done, e + 1)
                nc.scalar.activation(ring_h[slot], raw_slot[slot].rearrange("p (a b) -> p a b", a=2),
                                     ACT.Copy).then_inc(hi_done, 1)

            def ent_head(l):
                for j in range(RING):
                    ent_high(j, l * FT + j, raw_value(at["E", l, j]))

            def ent_loop(l):
                with act.Fori(0, FT // RING - 1) as i:
                    for j in range(RING):
                        ent_high(j, l * FT + RING + j + i * RING, raw_value(at["E", l, RING]) + i * 16)

            def stage_sum(u, source):
                nc.scalar.activation(tile[u % 2], source, ACT.Copy,
                                     accum_out=rowsum[:, u:u + 1]).then_inc(summed, 1)

            def stage_high(u, st, k):
                gain = gain_col(st, k)
                act.wait_ge(centred, u + 1)
                nc.scalar.activation(stage_h[:, st, k, :], tile[u % 2], ACT.Copy,
                                     scale=1.0 if gain is None else gain).then_inc(stage_hi, 1)

            def path_tiles(l):
                for k in range(KT + 1):
                    if k < KT:
                        act.wait_ge(scaled, PATH_U[l] + k + 1)
                        stage_sum(PATH_U[l] + k, tile[k % 2])
                    if k:
                        stage_high(PATH_U[l] + k - 1, 2 * l + 1, k - 1)

            def ent_tiles(l):
                act.wait_ge(step_done, KT + (l + 1) * FT)
                for k in range(KT + 1):
                    if k < KT:
                        act.wait_ge(stage_done, ENT_U[l] + k - 1)
                        stage_sum(ENT_U[l] + k, bank[fold_bank(l, k)][:, :])
                    if k:
                        stage_high(ENT_U[l] + k - 1, 2 * l, k - 1)

            def lora_high(bb, c, place):
                act.wait_ge(lsum_done, bb * ITEMS + c + 1)
                if c == 0:
                    nc.scalar.activation(am_h[:, :], place[0], ACT.Copy).then_inc(lhi, 1)
                else:
                    h, k = divmod(c - 1, KT)
                    nc.scalar.activation(mb_h[:, k, h * D:(h + 1) * D], place[c % 2], ACT.Copy).then_inc(lhi, 1)

            def x_high(bb, half):
                act.wait_ge(x_in, bb * 16 + 16)
                nc.scalar.activation(x_h[:, 2 * half:2 * half + 2, :], amp[:, 2 * half:2 * half + 2, :],
                                     ACT.Copy).then_inc(xhi, 1)

            ent_head(0)
            act.wait_ge(step_done, KT)
            for m in range(KT):
                nc.scalar.activation(fold[:, m, 0:D], bank[m][:, :], ACT.Copy).then_inc(m_act, 1)
            for h in range(2):
                act.wait_ge(q_mm, h + 1)
                nc.scalar.activation(q_h[:, h * D:(h + 1) * D], bank[h][:, :], ACT.Copy).then_inc(q_hi, 1)
            act.wait_ge(mod_mm, 1)
            for p in range(2):
                nc.scalar.activation(mod[:, p, :], bank[2 + p][:, :], ACT.Copy).then_inc(mod_in, 1)
            path_tiles(0)
            for c in range(ITEMS):
                lora_high(0, c, lsum_first)
            x_high(0, 0)
            x_high(0, 1)
            ent_loop(0)
            act.wait_ge(mod_mm, 2)
            act.wait_ge(scaled, KT)
            for p in range(2):
                nc.scalar.activation(mod[:, p, :], bank[p][:, :], ACT.Copy).then_inc(mod_in, 1)
            path_tiles(1)
            ent_head(1)
            ent_tiles(0)
            ent_loop(1)
            ent_tiles(1)

            def gate(bb, s, source):
                m = s % KT
                act.wait_ge(s_mm, bb * NSLICE + s + 1)
                if s < KT:
                    nc.scalar.activation(amp[:, m, :], source, ACT.Sigmoid,
                                         bias=col[:, AMP_B + m:AMP_B + m + 1]).then_inc(s_act, 1)
                else:
                    nc.scalar.activation(work[:, m, :], source, ACT.Tanh,
                                         bias=col[:, PH_B + m:PH_B + m + 1]).then_inc(s_act, 1)
                    if m:
                        turn_abs(bb, m - 1)

            def turn_abs(bb, m):
                act.wait_ge(s_act, bb * NSLICE + KT + m + 1)
                nc.scalar.activation(work[:, m, :], work[:, m, :], ACT.Abs,
                                     bias=minus_quarter[:, :]).then_inc(abs_done, 1)

            def h_sin(bb, m):
                act.wait_ge(abs_done, bb * KT + m + 1)
                nc.scalar.activation(work[:, m, :], work[:, m, :], ACT.Sin, scale=-math.pi,
                                     bias=half_pi[:, :]).then_inc(sin_done, 1)

            def h_high(bb, m):
                act.wait_ge(h_done, bb * KT + m + 1)
                nc.scalar.activation(h_h[:, m, :], work[:, m, :], ACT.Copy).then_inc(hhi, 1)

            def h_all(bb):
                turn_abs(bb, KT - 1)
                for m in range(KT + 1):
                    if m < KT:
                        h_sin(bb, m)
                    if m:
                        h_high(bb, m - 1)

            for s in range(NSLICE):
                if s == KT:
                    act.wait_ge(stage_done, 4 * KT)
                gate(0, s, bank[(s + 4) % 8][:, :])
            h_all(0)
            for st in range(STAGES):
                act.wait_ge(bias_mm, st + 1)
                nc.scalar.activation(bias[:, st, :], bank[4 + st][:, :], ACT.Copy,
                                     accum_out=rowsum[:, 16 + st:17 + st]).then_inc(bias_sum, 1)

            def z_high(b, st, i):
                t = st * NT + i
                act.wait_ge(t_mm, b * 12 + t + 1)
                nc.scalar.activation(z_h[:, :, i * P:(i + 1) * P],
                                     bank[4 + t % 2][:, :].rearrange("p (k t) -> p k t", k=KT),
                                     ACT.Copy).then_inc(zhi, 1)

            def square(b, st, i):
                n = st * NT + i
                if n:
                    act.wait_ge(sq_done, b * 16 + n)
                act.wait_ge(v_done, b * 16 + n + 1 + STAGES)
                nc.scalar.activation(junk[:, :], work[:, i, :], ACT.Square,
                                     accum_out=sumsq[:, n:n + 1]).then_inc(sq_done, 1)

            def batch(b, with_next):
                seq = order(with_next)
                for pos, (kind, one, two) in enumerate(seq):
                    if pos >= LAG and transposed(seq[pos - LAG]):
                        z_high(b, *seq[pos - LAG][1:])
                    if kind == "Y":
                        square(b, one, two)
                    else:
                        gate(b + 1, one, bank[one % KT][:, :])
                    if with_next:
                        if pos == 0:
                            lora_high(b + 1, 0, lsum)
                        if LORA_AT <= pos < LORA_AT + NSLICE:
                            lora_high(b + 1, pos - LORA_AT + 1, lsum)
                        if pos in X_AT:
                            x_high(b + 1, pos - X_AT[0])
                    if kind == "S" and one == NSLICE - 1:
                        h_all(b + 1)

            with act.Fori(0, B - 1) as b:
                batch(b, True)
            batch(B - 1, False)

        @block.vector
        def _(dve):
            own = Tally(dve_chain)
            ph, kk = gb[0:4, 0, :], work[0:4, 0, :]

            dve.wait_ge(rows_in, 32)
            own.inc(nc.vector.tensor_scalar(kk, ph, 1.0 / (2 * math.pi), ROUND, ALU.mult, ALU.add), dve)
            own.inc(nc.vector.tensor_scalar(kk, kk, ROUND, None, ALU.subtract), dve)
            for part in TWO_PI:
                own.inc(nc.vector.scalar_tensor_tensor(ph, kk, -part, ph, ALU.mult, ALU.add), dve)
            nc.vector.tensor_scalar(ph, ph, PI_BELOW, -PI_BELOW, ALU.min, ALU.max).then_inc(reduced, 1)

            def fold_low(k):
                dve.wait_ge(hi_done, k + 1)
                nc.vector.tensor_tensor(x_l[:, k, :], amp[:, k, :], x_h[:, k, :].bitcast(F32), ALU.subtract)
                nc.vector.tensor_tensor(mb_l[:, k, :], fold[:, k, :], mb_h[:, k, :].bitcast(F32),
                                        ALU.subtract).then_inc(lo_done, 1)

            dve.wait_ge(trig, 2)
            dve.wait_ge(const_done, 5)
            nc.vector.tensor_tensor(mod_rows, work[0:4, 1, :], work[0:4, 0, :], ALU.add).then_inc(rows_done, 1)
            for l in range(L):
                own.inc(nc.vector.tensor_tensor(layer_rows[:, l:l + 1], ident[:, 2 * l:2 * l + 1],
                                                ident[:, 2 * l + 1:2 * l + 2], ALU.add), dve)
            dve.wait_ge(rows_done, 1)
            for l in range(L):
                nc.vector.scalar_tensor_tensor(bias[0:4, 2 * l + 1, :], gb[0:4, 1, :], layer_rows[0:4, l:l + 1],
                                               mod_rows, ALU.mult, ALU.mult).then_inc(rows_done, 1)

            dve.wait_ge(small_in, 32)
            own.inc(nc.vector.tensor_copy(idx_f[:, :], idx_i[:, :]), dve)
            own.inc(nc.vector.tensor_copy(pcol[:, :], pcol_i[:, :]), dve)
            own.inc(nc.vector.tensor_scalar(idx_f[:, :], idx_f[:, :], -float(RANK), pcol[:, :], ALU.mult, ALU.add), dve)
            own.inc(nc.vector.tensor_scalar(tmp4[:, :], idx_f[:, :], 0.0, None, ALU.is_ge), dve)
            own.inc(nc.vector.scalar_tensor_tensor(tmp4[:, :], idx_f[:, :], float(RANK), tmp4[:, :],
                                                   ALU.is_lt, ALU.mult), dve)
            own.inc(nc.vector.tensor_scalar(pick[:, :], tmp4[:, :], col[:, SCALE:SCALE + 1], None, ALU.mult), dve)

            for k in range(KT):
                fold_low(k)
            dve.wait_ge(b_hi, 1)
            nc.vector.tensor_tensor(am_l[:, :], b_raw, am_h[:, :].bitcast(F32), ALU.subtract).then_inc(b_lo, 1)

            dve.wait_ge(entpb_in, 32)
            dve.wait_ge(rows_done, L + 1)
            nc.vector.memset(negmean[:, :], 0.0).then_inc(acc_done, 1)

            def ent_low(slot, l, e, column):
                raw2 = raw_slot[slot].rearrange("p (a b) -> p a b", a=2)
                dve.wait_ge(hi_done, KT + e + 1)
                nc.vector.tensor_tensor(ring_l[slot], raw2, ring_h[slot].bitcast(F32),
                                        ALU.subtract).then_inc(lo_done, 1)
                dve.wait_ge(acc_done, e + 1)
                nc.vector.scalar_tensor_tensor(bias[:, 2 * l, :], raw2[:, 1, :], column, bias[:, 2 * l, :],
                                               ALU.mult, ALU.add).then_inc(acc_done, 1)

            def ent_head(l):
                for j in range(RING):
                    c = ENT_B + l * FT + j
                    ent_low(j, l, l * FT + j, col[:, c:c + 1])

            def ent_loop(l):
                with dve.Fori(0, FT // RING - 1) as i:
                    for j in range(RING):
                        ent_low(j, l, l * FT + RING + j + i * RING,
                                col[:, bass.ds(ENT_B + l * FT + RING + j + i * RING, 1)])

            def stage_tile(u, st, k):
                t = tile[u % 2]
                gain, shift = gain_col(st, k), shift_col(st, k)
                dve.wait_ge(summed, u + 1)
                nc.vector.tensor_scalar(negmean[:, u:u + 1], rowsum[:, u:u + 1], -1.0 / D, -1.0 / D,
                                        ALU.mult, ALU.add)
                own.inc(nc.vector.tensor_tensor(t[:, k * P:(k + 1) * P], t[:, k * P:(k + 1) * P],
                                                ident[:, :], ALU.add), dve)
                nc.vector.tensor_scalar(t, t, negmean[:, u:u + 1], None, ALU.add).then_inc(centred, 1)
                if shift is not None:
                    dve.wait_ge(centred, u + 1)
                    own.inc(nc.vector.scalar_tensor_tensor(bias[:, st, :], t, shift, bias[:, st, :],
                                                           ALU.mult, ALU.add), dve)
                dve.wait_ge(stage_hi, u + 1)
                high = stage_h[:, st, k, :].bitcast(F32)
                if gain is None:
                    low = nc.vector.tensor_tensor(stage_l[:, st, k, :], t, high, ALU.subtract)
                else:
                    low = nc.vector.scalar_tensor_tensor(stage_l[:, st, k, :], t, gain, high,
                                                         ALU.mult, ALU.subtract)
                low.then_inc(stage_done, 1)

            def lora_sum(bb, c, place, source):
                if c == 0:
                    nc.vector.tensor_scalar(place[0], a_all[:, :], pick[:, bass.ds(bb, 1)], None,
                                            ALU.mult).then_inc(lsum_done, 1)
                else:
                    h, k = divmod(c - 1, KT)
                    dve.wait_ge(l_mm, bb * NSLICE + c)
                    nc.vector.tensor_tensor(place[c % 2], source, fold[:, k, h * D:(h + 1) * D],
                                            ALU.add).then_inc(lsum_done, 1)

            def lora_low(bb, c, place):
                dve.wait_ge(lhi, bb * ITEMS + c + 1)
                if c == 0:
                    low, high = am_l[:, :], am_h[:, :]
                else:
                    h, k = divmod(c - 1, KT)
                    low, high = mb_l[:, k, h * D:(h + 1) * D], mb_h[:, k, h * D:(h + 1) * D]
                nc.vector.tensor_tensor(low, place[c % 2], high.bitcast(F32), ALU.subtract).then_inc(llo, 1)

            def x_low(bb, half):
                s = slice(2 * half, 2 * half + 2)
                dve.wait_ge(xhi, bb * 2 + half + 1)
                nc.vector.tensor_tensor(x_l[:, s, :], amp[:, s, :], x_h[:, s, :].bitcast(F32),
                                        ALU.subtract).then_inc(xlo, 1)

            ent_head(0)
            dve.wait_ge(step_done, KT)
            for m in range(KT):
                nc.vector.tensor_copy(fold[:, m, D:2 * D], bank[KT + m][:, :]).then_inc(m_dve, 1)
            for h in range(2):
                dve.wait_ge(q_hi, h + 1)
                nc.vector.tensor_tensor(q_l[:, h * D:(h + 1) * D], bank[h][:, :],
                                        q_h[:, h * D:(h + 1) * D].bitcast(F32), ALU.subtract).then_inc(q_lo, 1)
            for k in range(KT):
                stage_tile(PATH_U[0] + k, 1, k)
            dve.wait_ge(a_in, 16)
            dve.wait_ge(m_act, KT)
            for c in range(ITEMS):
                lora_sum(0, c, lsum_first, bank[2 + (c - 1) % 2][:, :])
                lora_low(0, c, lsum_first)
            x_low(0, 0)
            x_low(0, 1)
            ent_loop(0)
            for k in range(KT):
                stage_tile(PATH_U[1] + k, 3, k)
            ent_head(1)
            for k in range(KT):
                stage_tile(ENT_U[0] + k, 0, k)
            ent_loop(1)
            for k in range(KT):
                stage_tile(ENT_U[1] + k, 2, k)

            def h_all(bb):
                for m in range(KT + 1):
                    if m < KT:
                        dve.wait_ge(sin_done, bb * KT + m + 1)
                        nc.vector.scalar_tensor_tensor(work[:, m, :], work[:, m, :], math.sqrt(2), amp[:, m, :],
                                                       ALU.mult, ALU.mult).then_inc(h_done, 1)
                    if m:
                        dve.wait_ge(hhi, bb * KT + m)
                        nc.vector.tensor_tensor(h_l[:, m - 1, :], work[:, m - 1, :],
                                                h_h[:, m - 1, :].bitcast(F32), ALU.subtract).then_inc(hlo, 1)

            h_all(0)
            for st in range(STAGES):
                dve.wait_ge(bias_sum, st + 1)
                c = slice(16 + st, 17 + st)
                own.inc(nc.vector.tensor_scalar(negmean[:, c], rowsum[:, c], -1.0 / D, None, ALU.mult), dve)
                nc.vector.tensor_scalar(bias[:, st, :], bias[:, st, :], negmean[:, c], None,
                                        ALU.add).then_inc(v_done, 1)
            dve.wait_ge(v_done, STAGES)

            def stage_out(b, st, i):
                n = st * NT + i
                dve.wait_ge(y_mm, b * 16 + n + 1)
                if st == 0:
                    nc.vector.tensor_tensor(work[:, i, :], bank[i][:, :], bias[:, st, :],
                                            ALU.add).then_inc(v_done, 1)
                else:
                    dve.wait_ge(r_done, b * 16 + n - NT + 1)
                    nc.vector.scalar_tensor_tensor(work[:, i, :], bank[i][:, :], rstd[:, n - NT:n - NT + 1],
                                                   bias[:, st, :], ALU.mult, ALU.add).then_inc(v_done, 1)

            def z_low(b, st, i):
                t = st * NT + i
                dve.wait_ge(zhi, b * 12 + t + 1)
                nc.vector.tensor_tensor(z_l[:, :, i * P:(i + 1) * P],
                                        bank[4 + t % 2][:, :].rearrange("p (k t) -> p k t", k=KT),
                                        z_h[:, :, i * P:(i + 1) * P].bitcast(F32), ALU.subtract).then_inc(zlo, 1)

            def finish(b, i):
                n = (STAGES - 1) * NT + i
                dve.wait_ge(r_done, b * 16 + n + 1)
                own.inc(nc.vector.scalar_tensor_tensor(work[:, i, :], work[:, i, :], rstd[:, n:n + 1], gb[:, 0, :],
                                                       ALU.mult, ALU.mult), dve)
                dve.wait_ge(res_done, b * NT + i + 1)
                nc.vector.tensor_tensor(res[:, i, :], work[:, i, :], res[:, i, :], ALU.add).then_inc(out_done, 1)

            def batch(b, with_next):
                seq = order(with_next)
                for pos, (kind, one, two) in enumerate(seq):
                    if kind == "Y":
                        stage_out(b, one, two)
                        if one == STAGES - 1 and two:
                            finish(b, two - 1)
                    if pos >= LAG and transposed(seq[pos - LAG]):
                        z_low(b, *seq[pos - LAG][1:])
                    if with_next:
                        c = 0 if pos == 0 else pos - LORA_AT + 1
                        if pos == 0 or LORA_AT <= pos < LORA_AT + NSLICE:
                            lora_sum(b + 1, c, lsum, bank[6 + (c - 1) % 2][:, :])
                            lora_low(b + 1, c, lsum)
                        if pos in X_AT:
                            x_low(b + 1, pos - X_AT[0])
                    if kind == "S" and one == NSLICE - 1:
                        h_all(b + 1)
                finish(b, NT - 1)

            with dve.Fori(0, B - 1) as b:
                own.enter(b * NT)
                batch(b, True)
            own.leave(B - 1)
            batch(B - 1, False)

        @block.tensor
        def _(pe):
            def split_product(dst, parts):
                passes = [(a, b) for lh, ll, rh, rl in parts for a, b in ((lh, rh), (lh, rl), (ll, rh))]
                for n, (a, b) in enumerate(passes):
                    last = nc.tensor.matmul(dst, a, b, start=n == 0, stop=n == len(passes) - 1)
                return last

            def fold_step(slot_h, slot_l, rhs_h, rhs_l, banks, first, final):
                for m in range(KT):
                    s = slice(m * P, (m + 1) * P)
                    for q, bk in enumerate(banks[m]):
                        c = slice(q * D, (q + 1) * D)
                        passes = ((slot_h[:, s], rhs_h[:, c]), (slot_h[:, s], rhs_l[:, c]), (slot_l[:, s], rhs_h[:, c]))
                        for n, (a, b) in enumerate(passes):
                            last = nc.tensor.matmul(bank[bk][:, :], a, b, start=first and n == 0,
                                                    stop=final and n == 2)
                last.then_inc(step_done, 1)

            for k in range(KT):
                pe.wait_ge(lo_done, k + 1)
                fold_step(x_h[:, k, :], x_l[:, k, :], mb_h[:, k, :], mb_l[:, k, :],
                          [(m, KT + m) for m in range(KT)], k == 0, k == KT - 1)
            pe.wait_ge(b_lo, 1)
            for h in range(2):
                pe.wait_ge(m_act, h + 1)
                c = slice(h * D, (h + 1) * D)
                split_product(bank[h][:, :], [
                    (am_h[:, k * P:(k + 1) * P], am_l[:, k * P:(k + 1) * P], mb_h[:, k, c], mb_l[:, k, c])
                    for k in range(KT)]).then_inc(q_mm, 1)

            def spread_mod(l, first_bank):
                for p in range(2):
                    row = 2 * l + p
                    last = nc.tensor.matmul(bank[first_bank + p][:, :], ident[0:4, row:row + 1].to_broadcast([4, P]),
                                            mod_rows, start=True, stop=True)
                last.then_inc(mod_mm, 1)

            def ent_step(l, j, value, first, final):
                pe.wait_ge(lo_done, value)
                fold_step(ring_h[j][:, 0, :], ring_l[j][:, 0, :], ring_h[j][:, 1, :], ring_l[j][:, 1, :],
                          [(fold_bank(l, m),) for m in range(KT)], first, final)

            def ent_head(l):
                for j in range(RING):
                    ent_step(l, j, KT + l * FT + j + 1, j == 0, False)

            def ent_loop(l):
                with pe.Fori(0, FT // RING - 2) as i:
                    for j in range(RING):
                        ent_step(l, j, KT + l * FT + RING + j + 1 + i * RING, False, False)
                for j in range(RING):
                    ent_step(l, j, KT + (l + 1) * FT - RING + j + 1, False, j == RING - 1)

            def lora_product(bb, c, dst):
                h, k = divmod(c - 1, KT)
                s, q = slice(k * P, (k + 1) * P), slice(h * D, (h + 1) * D)
                split_product(dst, [(am_h[:, s], am_l[:, s], q_h[:, q], q_l[:, q])]).then_inc(l_mm, 1)

            pe.wait_ge(rows_done, 1)
            pe.wait_ge(m_act, KT)
            spread_mod(0, 2)
            pe.wait_ge(m_dve, KT)
            ent_head(0)
            pe.wait_ge(q_lo, 2)
            spread_mod(1, 0)
            pe.wait_ge(mod_in, 2)
            pe.wait_ge(llo, 1)
            for c in range(1, ITEMS):
                if c > 2:
                    pe.wait_ge(lsum_done, c - 1)
                lora_product(0, c, bank[2 + (c - 1) % 2][:, :])
            ent_loop(0)
            pe.wait_ge(mod_in, 4)
            pe.wait_ge(lsum_done, ITEMS)
            ent_head(1)
            ent_loop(1)

            def slice_product(bb, s, dst):
                h, m = divmod(s, KT)
                c = slice(h * D + m * P, h * D + (m + 1) * P)
                if s == 0:
                    pe.wait_ge(xlo, bb * 2 + 2)
                    pe.wait_ge(llo, bb * ITEMS + 1 + KT)
                if s == KT:
                    pe.wait_ge(llo, bb * ITEMS + ITEMS)
                split_product(dst, [(mb_h[:, k, c], mb_l[:, k, c], x_h[:, k, :], x_l[:, k, :])
                                    for k in range(KT)]).then_inc(s_mm, 1)

            pe.wait_ge(summed, ENT_U[0] + KT)
            for s in range(NSLICE):
                if s == KT:
                    pe.wait_ge(summed, ENT_U[1] + KT)
                slice_product(0, s, bank[(s + 4) % 8][:, :])
            pe.wait_ge(stage_done, 16)
            pe.wait_ge(s_act, KT)
            for st in range(STAGES):
                nc.tensor.matmul(bank[4 + st][:, :], ones[:, :], bias[:, st, :], start=True,
                                 stop=True).then_inc(bias_mm, 1)

            def stage_product(b, st, i, with_next):
                n = st * NT + i
                s = slice(i * P, (i + 1) * P)
                if st == 0:
                    if i == 0:
                        pe.wait_ge(s_act, b * NSLICE + NSLICE)
                        pe.wait_ge(hlo, b * KT + KT)
                    src_h, src_l = h_h, h_l
                else:
                    pe.wait_ge(zlo, b * 12 + n - NT + 1)
                    src_h, src_l = z_h, z_l
                pe.wait_ge(v_done, b * 16 + n + 1)
                if st == STAGES - 1 and with_next:
                    pe.wait_ge(s_act, b * NSLICE + NSLICE + KT + i + 1)
                split_product(bank[i][:, :], [(src_h[:, k, s], src_l[:, k, s], stage_h[:, st, k, :],
                                               stage_l[:, st, k, :]) for k in range(KT)]).then_inc(y_mm, 1)

            def transpose_tile(b, st, i):
                t = st * NT + i
                pe.wait_ge(v_done, b * 16 + t + 1 + STAGES)
                if t >= 2:
                    pe.wait_ge(zlo, b * 12 + t - 1)
                for k in range(KT):
                    last = nc.tensor.transpose(bank[4 + t % 2][:, k * P:(k + 1) * P], work[:, i, k * P:(k + 1) * P],
                                               ident[:, :])
                last.then_inc(t_mm, 1)

            def batch(b, with_next):
                seq = order(with_next)
                for pos, (kind, one, two) in enumerate(seq):
                    if kind == "Y":
                        stage_product(b, one, two, with_next)
                    else:
                        if one < KT:
                            pe.wait_ge(v_done, b * 16 + 2 * NT + one + 1 + STAGES)
                        else:
                            pe.wait_ge(s_act, b * NSLICE + NSLICE + one - KT + 1)
                        slice_product(b + 1, one, bank[one % KT][:, :])
                    if pos >= LAG and transposed(seq[pos - LAG]):
                        transpose_tile(b, *seq[pos - LAG][1:])
                    if with_next and LORA_AT <= pos < LORA_AT + NSLICE:
                        c = pos - LORA_AT + 1
                        pe.wait_ge(llo, (b + 1) * ITEMS + 1)
                        if c > 2:
                            pe.wait_ge(lsum_done, (b + 1) * ITEMS + c - 1)
                        lora_product(b + 1, c, bank[6 + (c - 1) % 2][:, :])

            with pe.Fori(0, B - 1) as b:
                batch(b, True)
            batch(B - 1, False)


def kernel(**inputs):
    import numpy as np
    import concourse.bacc as bacc
    from concourse.bass_utils import run_bass_kernel_spmd

    def a(name):
        return np.asarray(inputs[name])

    def columns(v, tiles):
        return v.reshape(-1, tiles, P).transpose(2, 0, 1).reshape(P, -1)

    f = lambda name: a("L0_ffn_" + name)
    x = a("x")
    tokens = x.reshape(B, P, NT, D)
    arrays = {
        "xt": tokens.reshape(B, P, NT, KT, P).transpose(0, 4, 3, 2, 1).reshape(B, P, KT, T),
        "xr": tokens,
        "wc": a("L0_cond_W").reshape(KT, P, D),
        "ap": np.concatenate([f("amp_w"), f("ph_w")], axis=1).reshape(KT, P, 2 * D),
        "bt": a("L0_cond_Bm").reshape(NADAPT, KT, P, RANK).transpose(2, 1, 0, 3).reshape(P, KT * NADAPT * RANK),
        "aa": a("L0_cond_A").reshape(NADAPT * RANK, D),
        "idx": a("itok_B_0_6"),
        "cols": np.concatenate([
            columns(f("amp_b"), KT), columns(f("ph_b"), KT), columns(f("ent_b"), FT),
            columns(f("ln3_g"), KT), columns(f("ln3_b"), KT), columns(f("ln4_g"), KT), columns(f("ln4_b"), KT),
            np.repeat(a("L0_cond_scalings"), RANK).reshape(P, 1)], axis=1),
        "phase": f("phase").reshape(L * 2, D),
        "pathb": f("path_b").reshape(L * 2, D),
        "entpb": f("ent_pb"),
        "gb_rows": np.stack([f("ln4_g")[L - 1], f("ln4_b")[L - 1]]),
        "ent": np.concatenate([f("ent_w").transpose(0, 2, 1), f("ent_pw")], axis=2).reshape(L, FT, P, 2 * D),
        "path": f("path_w").reshape(L, 2, KT, P, D).transpose(0, 2, 3, 1, 4).reshape(L, KT, P, 2 * D),
    }
    nc = bacc.Bacc("TRN2", target_bir_lowering=False, num_devices=1, dynamic_dma_scratch_size=1024)
    sent, args = {}, []
    for name, v in arrays.items():
        v = np.ascontiguousarray(v)
        sent["in_" + name] = v
        args.append(nc.dram_tensor("in_" + name, v.shape, mybir.dt.from_np(v.dtype), kind="ExternalInput").ap())
    out = nc.dram_tensor("out_0", (B, P, NT, D), F32, kind="ExternalOutput").ap()
    build(nc, *args, out)
    r = run_bass_kernel_spmd(nc, [sent], core_ids=[0])
    return r.results[0]["out_0"].reshape(B, T, D)
```

```python
import concourse.bass as bass
from concourse import mybir
from contextlib import ExitStack
import math

F32 = mybir.dt.float32
F32R = mybir.dt.float32r
I32 = mybir.dt.int32
ACT = mybir.ActivationFunctionType
ALU = mybir.AluOpType

P = 128
D = 512
B = 4
T = 512
KT = D // P
NT = T // P
L = 2
F = 2048
FT = F // P
NADAPT, RANK = 8, 16
EPS = 1e-5
STAGES = 2 * L
RING = 4
PATH_WITH = 2
NSLICE = 8

AMP_B, PH_B = 0, KT
ENT_B = 2 * KT
LN3_G = ENT_B + L * FT
LN3_B = LN3_G + L * KT
LN4_G = LN3_B + L * KT
LN4_B = LN4_G + L * KT
SCALE = LN4_B + L * KT
NCOLS = SCALE + 1


ROUND = 1.5 * 2 ** 23
TWO_PI = [6.28125, round((2 * math.pi - 6.28125) * 2 ** 20) / 2 ** 20]
TWO_PI.append(2 * math.pi - sum(TWO_PI))
PI_BELOW = 3.1415925


class Tally:

    def __init__(self, sem):
        self.sem, self.count, self.loop = sem, 0, 0

    def enter(self, loop):
        self.loop, self.start = loop, self.count

    def leave(self, iterations):
        self.loop, self.count = 0, self.start + iterations * (self.count - self.start)

    def inc(self, instruction, engine=None):
        self.count += 1
        instruction.then_inc(self.sem, 1)
        if engine is not None:
            engine.wait_ge(self.sem, self.loop + self.count)


def build(nc, xt, xr, wc, ap, bt, aa, idx, cols, phase, pathb, entpb, gb_rows, ent, path, out):
    ctx = ExitStack()
    with ctx:
        def sb(name, shape, dt=F32):
            return ctx.enter_context(nc.sbuf_tensor(name, shape, dt))

        def sem(name):
            return ctx.enter_context(nc.semaphore(name))

        stage_h = sb("stage_h", [P, STAGES, KT, D], F32R)
        stage_l = sb("stage_l", [P, STAGES, KT, D], F32R)
        fold = sb("fold", [P, KT, 2 * D])
        q_h = sb("q_h", [P, 2 * D], F32R)
        q_l = sb("q_l", [P, 2 * D], F32R)
        bias = sb("bias", [P, STAGES, D])
        gb = sb("gb", [P, 2, D])
        a_all = sb("a_all", [P, D])
        col = sb("col", [P, NCOLS])
        ident = sb("ident", [P, P])
        ones = sb("ones", [P, P])
        mb_h = sb("mb_h", [P, KT, 2 * D], F32R)
        mb_l = sb("mb_l", [P, KT, 2 * D], F32R)
        x_h = sb("x_h", [P, KT, T], F32R)
        x_l = sb("x_l", [P, KT, T], F32R)
        am_h = sb("am_h", [P, D], F32R)
        am_l = sb("am_l", [P, D], F32R)
        h_h = sb("h_h", [P, KT, T], F32R)
        h_l = sb("h_l", [P, KT, T], F32R)
        z_h = sb("z_h", [P, KT, T], F32R)
        z_l = sb("z_l", [P, KT, T], F32R)
        amp = sb("amp", [P, KT, T])
        work = sb("work", [P, NT, D])
        mod = sb("mod", [P, 2, D])
        raw = sb("raw", [P, 3, 2 * D])
        junk = sb("junk", [P, D])
        idx_i = sb("idx_i", [P, B], I32)
        idx_f = sb("idx_f", [P, B])
        pcol_i = sb("pcol_i", [P, 1], I32)
        pcol = sb("pcol", [P, 1])
        pick = sb("pick", [P, B])
        tmp4 = sb("tmp4", [P, B])
        rowsum = sb("rowsum", [P, 16 + STAGES])
        negmean = sb("negmean", [P, 16 + STAGES])
        layer_rows = sb("layer_rows", [P, L])
        half_pi = sb("half_pi", [P, 1])
        minus_quarter = sb("minus_quarter", [P, 1])
        sumsq = sb("sumsq", [P, 16])
        var = sb("var", [P, 16])
        minus_half = sb("minus_half", [P, 2])
        eps_sum = sb("eps_sum", [P, 2])
        newton_a = sb("newton_a", [P, 2])
        newton_b = sb("newton_b", [P, 2])
        root = sb("root", [P, 16])
        corr = sb("corr", [P, 16])
        rstd = sb("rstd", [P, 16])

        bank = [ctx.enter_context(nc.psum_tensor(f"bank{i}", [P, 512], F32)) for i in range(8)]

        raw_slot = [raw[:, 0, :], raw[:, 1, :], raw[:, 2, :],
                    work[:, 0:2, :].rearrange("p a b -> p (a b)")]
        ring_h = [h_h[:, 0:2, :], h_h[:, 2:4, :], z_h[:, 0:2, :], z_h[:, 2:4, :]]
        ring_l = [h_l[:, 0:2, :], h_l[:, 2:4, :], z_l[:, 0:2, :], z_l[:, 2:4, :]]
        tile = [work[:, 2, :], work[:, 3, :]]
        b_raw = work[:, 2, :]
        lsum = [raw[:, 2, 0:D], raw[:, 2, D:2 * D]]
        turn = [mod[:, 0, :], mod[:, 1, :], lsum[0], lsum[1]]
        res = raw[:, 0:2, :].rearrange("p a (b c) -> p (a b) c", b=2)
        lsum_first = tile
        mod_rows = junk[0:4, :]

        fold_in = [sem(f"fold_in{k}") for k in range(KT)]
        small_in = sem("small_in")
        rows_in = sem("rows_in")
        entpb_in = sem("entpb_in")
        b_in = sem("b_in")
        a_in = sem("a_in")
        gb_in = sem("gb_in")
        raw_in = [sem(f"raw_in{s}") for s in range(RING)]
        x_in = sem("x_in")
        res_in = sem("res_in")
        stored = [sem(f"stored{i}") for i in range(NT)]
        const_done = sem("const_done")
        pool_chain = sem("pool_chain")
        dve_chain = sem("dve_chain")
        act_chain = sem("act_chain")
        reduced = sem("reduced")
        trig = sem("trig")
        rows_done = sem("rows_done")
        hi_done = sem("hi_done")
        lo_done = sem("lo_done")
        step_done = sem("step_done")
        acc_done = sem("acc_done")
        b_hi = sem("b_hi")
        b_lo = sem("b_lo")
        m_act = sem("m_act")
        m_dve = sem("m_dve")
        q_mm = sem("q_mm")
        q_hi = sem("q_hi")
        q_lo = sem("q_lo")
        mod_mm = sem("mod_mm")
        mod_in = sem("mod_in")
        scaled = sem("scaled")
        summed = sem("summed")
        centred = sem("centred")
        stage_hi = sem("stage_hi")
        stage_done = sem("stage_done")
        bias_mm = sem("bias_mm")
        bias_sum = sem("bias_sum")
        y_mm = sem("y_mm")
        s_mm = sem("s_mm")
        l_mm = sem("l_mm")
        t_mm = sem("t_mm")
        v_done = sem("v_done")
        sq_done = sem("sq_done")
        r_done = sem("r_done")
        zhi = sem("zhi")
        zlo = sem("zlo")
        lsum_done = sem("lsum_done")
        lhi = sem("lhi")
        llo = sem("llo")
        xhi = sem("xhi")
        xlo = sem("xlo")
        s_act = sem("s_act")
        abs_done = sem("abs_done")
        sin_done = sem("sin_done")
        h_done = sem("h_done")
        hhi = sem("hhi")
        hlo = sem("hlo")
        res_done = sem("res_done")
        out_done = sem("out_done")

        STEPS = []
        for l in range(L):
            for k in range(FT):
                if k // RING == PATH_WITH:
                    STEPS.append(("P", l, k % RING))
                STEPS.append(("E", l, k))
        at = {step: g for g, step in enumerate(STEPS)}

        def raw_value(g):
            return 16 * (g // RING + 1)

        def fold_bank(l, m):
            return 4 * (1 - l) + m

        def gain_col(st, k):
            if st == 0:
                return None
            base = LN3_G + (st // 2) * KT if st % 2 else LN4_G
            return col[:, base + k:base + k + 1]

        def shift_col(st, k):
            if st == 0:
                return None
            base = LN3_B + (st // 2) * KT if st % 2 else LN4_B
            return col[:, base + k:base + k + 1]

        PATH_U = [2 * l * KT for l in range(L)]
        ENT_U = [(2 * l + 1) * KT for l in range(L)]
        ITEMS = NSLICE + 1

        def order(with_next):
            y = [("Y", st, i) for st in range(STAGES) for i in range(NT)]
            s = [("S", s, 0) for s in range(NSLICE)] if with_next else []
            return y[:12] + s + y[12:]

        LAG = 2
        LORA_AT = 2
        X_AT = (7, 8)

        def transposed(item):
            return item[0] == "Y" and item[1] < STAGES - 1

        block = ctx.enter_context(nc.Block())

        @block.sync
        def _(sp):
            for k in range(KT):
                sp.dma_start(amp[:, k, :], wc[k]).then_inc(fold_in[k], 16)
                sp.dma_start(fold[:, k, :], ap[k]).then_inc(fold_in[k], 16)
            sp.dma_start(b_raw, bt).then_inc(b_in, 16)
            sp.dma_start(a_all[:, :], aa).then_inc(a_in, 16)
            for g, (kind, l, k) in enumerate(STEPS):
                if g == RING - 1:
                    sp.wait_ge(rows_done, L + 1)
                if g >= RING:
                    was, wl, wk = STEPS[g - RING]
                    if was == "E":
                        sp.wait_ge(acc_done, wl * FT + wk + 2)
                    else:
                        sp.wait_ge(scaled, wl * KT + wk + 1)
                sp.dma_start(raw_slot[g % RING], (ent if kind == "E" else path)[l, k]).then_inc(
                    raw_in[g % RING], 16)
                if g == 1:
                    sp.wait_ge(const_done, 2)
                    for layer in range(L):
                        sp.dma_start(bias[0:1, 2 * layer, :], entpb[layer:layer + 1, :]).then_inc(entpb_in, 16)
                if g == RING:
                    sp.wait_ge(lo_done, KT)
                    sp.dma_start(amp[:, :, :], xt[0]).then_inc(x_in, 16)
                    sp.dma_start(gb[:, :, :], gb_rows.partition_broadcast(P)).then_inc(gb_in, 16)

            def batch(b, with_next):
                if with_next:
                    sp.wait_ge(h_done, b * KT + KT)
                    sp.dma_start(amp[:, :, :], xt[bass.ds(b + 1, 1)].rearrange(
                        "a p k t -> (a p) k t")).then_inc(x_in, 16)
                for i in range(NT):
                    sp.wait_ge(out_done, b * NT + i + 1)
                    sp.dma_start(out[bass.ds(b, 1)].rearrange("a p t d -> (a p) t d")[:, i, :],
                                 res[:, i, :]).then_inc(stored[i], 16)
                if with_next:
                    for i in range(NT):
                        sp.wait_ge(stored[i], b * 16 + 16)
                    sp.dma_start(res, xr[bass.ds(b + 1, 1)].rearrange(
                        "a p t d -> (a p) t d")).then_inc(res_in, 16)

            sp.wait_ge(acc_done, L * FT + 1)
            sp.dma_start(res, xr[0]).then_inc(res_in, 16)
            with sp.Fori(0, B - 1) as b:
                batch(b, True)
            batch(B - 1, False)
            for i in range(NT):
                sp.wait_ge(stored[i], B * 16)

        @block.gpsimd
        def _(pool):
            own = Tally(pool_chain)
            own.inc(nc.gpsimd.memset(ident[:, :], 0.0), pool)
            nc.gpsimd.affine_select(out=ident[:, :], in_=ident[:, :], compare_op=ALU.not_equal, fill=1.0,
                                    base=0, pattern=[[-1, P]], channel_multiplier=1).then_inc(const_done, 1)
            nc.gpsimd.memset(bias[:, :, :], 0.0).then_inc(const_done, 1)
            nc.gpsimd.memset(half_pi[:, :], math.pi / 2).then_inc(const_done, 1)
            own.inc(nc.gpsimd.memset(minus_quarter[:, :], -0.25), pool)
            nc.gpsimd.iota(pcol_i[:, :], [[0, 1]], base=0, channel_multiplier=1).then_inc(const_done, 1)
            nc.gpsimd.memset(ones[:, :], 1.0).then_inc(const_done, 1)
            own.inc(nc.gpsimd.memset(minus_half[:, :], -0.5), pool)
            own.inc(nc.gpsimd.memset(eps_sum[:, :], D * EPS), pool)
            own.inc(nc.gpsimd.memset(newton_a[:, :], -0.5 * math.sqrt(D)), pool)
            own.inc(nc.gpsimd.memset(newton_b[:, :], 1.5 * math.sqrt(D)), pool)

            for l in range(L):
                pool.wait_ge(mod_in, 2 * (l + 1))
                for k in range(KT):
                    u = PATH_U[l] + k
                    g = at["P", l, k]
                    slot = raw_slot[g % RING].rearrange("p (a b) -> p a b", a=2)
                    pool.wait_ge(raw_in[g % RING], raw_value(g))
                    own.inc(nc.gpsimd.tensor_tensor(slot, slot, mod[:, :, :], ALU.mult), pool)
                    if u >= 2:
                        pool.wait_ge(stage_done, u - 1)
                    elif u == 0:
                        pool.wait_ge(llo, ITEMS)
                    nc.gpsimd.tensor_tensor(tile[u % 2], slot[:, 0, :], slot[:, 1, :],
                                            ALU.add).then_inc(scaled, 1)

            def token_scale(b, st, i):
                n = st * NT + i
                c = slice(n, n + 2)
                pool.wait_ge(sq_done, b * 16 + n + 2)
                own.inc(nc.gpsimd.tensor_tensor(var[:, c], sumsq[:, c], eps_sum[:, :], ALU.add), pool)
                own.inc(nc.gpsimd.tensor_tensor(root[:, c], var[:, c], minus_half[:, :], ALU.pow), pool)
                own.inc(nc.gpsimd.tensor_tensor(corr[:, c], root[:, c], root[:, c], ALU.mult), pool)
                own.inc(nc.gpsimd.tensor_tensor(corr[:, c], corr[:, c], var[:, c], ALU.mult), pool)
                own.inc(nc.gpsimd.tensor_tensor(corr[:, c], corr[:, c], newton_a[:, :], ALU.mult), pool)
                own.inc(nc.gpsimd.tensor_tensor(corr[:, c], corr[:, c], newton_b[:, :], ALU.add), pool)
                nc.gpsimd.tensor_tensor(rstd[:, c], root[:, c], corr[:, c], ALU.mult).then_inc(r_done, 1)

            pool.wait_ge(gb_in, 16)
            links = 6 * STAGES * NT // 2
            with pool.Fori(0, B) as b:
                own.enter(b * links)
                for st in range(STAGES):
                    token_scale(b, st, 0)
                    token_scale(b, st, 2)
                    if st == 0:
                        pool.wait_ge(res_in, b * 16 + 16)
                        for i in range(NT):
                            nc.gpsimd.tensor_tensor(res[:, i, :], res[:, i, :], gb[:, 1, :],
                                                    ALU.add).then_inc(res_done, 1)
            own.leave(B)

        @block.scalar
        def _(act):
            act.dma_start(gb[0:4, 0, :], phase).then_inc(rows_in, 16)
            act.dma_start(gb[0:4, 1, :], pathb).then_inc(rows_in, 16)
            act.dma_start(col[:, :], cols).then_inc(small_in, 16)
            act.dma_start(idx_i[:, :], idx.partition_broadcast(P)).then_inc(small_in, 16)

            for k in range(KT):
                act.wait_ge(fold_in[k], 32)
                nc.scalar.activation(x_h[:, k, :], amp[:, k, :], ACT.Copy)
                nc.scalar.activation(mb_h[:, k, :], fold[:, k, :], ACT.Copy).then_inc(hi_done, 1)
            act.wait_ge(b_in, 16)
            nc.scalar.activation(am_h[:, :], b_raw, ACT.Copy).then_inc(b_hi, 1)

            act.wait_ge(reduced, 1)
            nc.scalar.activation(work[0:4, 1, :], gb[0:4, 0, :], ACT.Sin).then_inc(trig, 1)
            nc.scalar.activation(work[0:4, 0, :], gb[0:4, 0, :], ACT.Abs).then_inc(act_chain, 1)
            act.wait_ge(act_chain, 1)
            act.wait_ge(const_done, 3)
            nc.scalar.activation(work[0:4, 0, :], work[0:4, 0, :], ACT.Sin, scale=-1.0,
                                 bias=half_pi[0:4, :]).then_inc(trig, 1)

            def ent_high(slot, e, source, landed):
                act.wait_ge(raw_in[source], landed)
                act.wait_ge(step_done, e + 1)
                nc.scalar.activation(ring_h[slot], raw_slot[source].rearrange("p (a b) -> p a b", a=2),
                                     ACT.Copy).then_inc(hi_done, 1)

            def ent_highs(l, first, count=RING):
                for k in range(first, first + count):
                    g = at["E", l, k]
                    ent_high(k % RING, l * FT + k, g % RING, raw_value(g))

            def stage_sum(u, source):
                nc.scalar.activation(tile[u % 2], source, ACT.Copy,
                                     accum_out=rowsum[:, u:u + 1]).then_inc(summed, 1)

            def stage_high(u, st, k):
                gain = gain_col(st, k)
                act.wait_ge(centred, u + 1)
                nc.scalar.activation(stage_h[:, st, k, :], tile[u % 2], ACT.Copy,
                                     scale=1.0 if gain is None else gain).then_inc(stage_hi, 1)

            def path_tile(l, k):
                act.wait_ge(scaled, l * KT + k + 1)
                stage_sum(PATH_U[l] + k, tile[k % 2])
                stage_high(PATH_U[l] + k, 2 * l + 1, k)

            def ent_tiles(l):
                act.wait_ge(step_done, KT + (l + 1) * FT)
                for k in range(KT + 1):
                    if k < KT:
                        act.wait_ge(stage_done, ENT_U[l] + k - 1)
                        stage_sum(ENT_U[l] + k, bank[fold_bank(l, k)][:, :])
                    if k:
                        stage_high(ENT_U[l] + k - 1, 2 * l, k - 1)

            def lora_high(bb, c, place):
                act.wait_ge(lsum_done, bb * ITEMS + c + 1)
                if c == 0:
                    nc.scalar.activation(am_h[:, :], place[0], ACT.Copy).then_inc(lhi, 1)
                else:
                    h, k = divmod(c - 1, KT)
                    nc.scalar.activation(mb_h[:, k, h * D:(h + 1) * D], place[c % 2], ACT.Copy).then_inc(lhi, 1)

            def x_high(bb, half):
                act.wait_ge(x_in, bb * 16 + 16)
                nc.scalar.activation(x_h[:, 2 * half:2 * half + 2, :], amp[:, 2 * half:2 * half + 2, :],
                                     ACT.Copy).then_inc(xhi, 1)

            ent_highs(0, 0)
            act.wait_ge(step_done, KT)
            for m in range(KT):
                nc.scalar.activation(fold[:, m, 0:D], bank[m][:, :], ACT.Copy).then_inc(m_act, 1)
            for h in range(2):
                act.wait_ge(q_mm, h + 1)
                nc.scalar.activation(q_h[:, h * D:(h + 1) * D], bank[h][:, :], ACT.Copy).then_inc(q_hi, 1)
            lora_high(0, 0, lsum_first)
            act.wait_ge(mod_mm, 1)
            for p in range(2):
                nc.scalar.activation(mod[:, p, :], bank[2 + p][:, :], ACT.Copy).then_inc(mod_in, 1)
            for j in range(RING):
                lora_high(0, 2 * j + 1, lsum_first)
                lora_high(0, 2 * j + 2, lsum_first)
                ent_highs(0, RING + j, 1)
            x_high(0, 0)
            x_high(0, 1)
            for l in range(L):
                if l:
                    ent_highs(l, 0)
                    ent_tiles(l - 1)
                    ent_highs(l, RING)
                for k in range(KT):
                    ent_highs(l, 2 * RING + k, 1)
                    path_tile(l, k)
                if l == 0:
                    act.wait_ge(mod_mm, 2)
                    for p in range(2):
                        nc.scalar.activation(mod[:, p, :], bank[p][:, :], ACT.Copy).then_inc(mod_in, 1)
                ent_highs(l, 3 * RING)
            ent_tiles(L - 1)

            def gate(bb, s, source):
                m = s % KT
                act.wait_ge(s_mm, bb * NSLICE + s + 1)
                if s < KT:
                    nc.scalar.activation(amp[:, m, :], source, ACT.Sigmoid,
                                         bias=col[:, AMP_B + m:AMP_B + m + 1]).then_inc(s_act, 1)
                else:
                    nc.scalar.activation(turn[m], source, ACT.Tanh,
                                         bias=col[:, PH_B + m:PH_B + m + 1]).then_inc(s_act, 1)
                    if m:
                        turn_abs(bb, m - 1)

            def turn_abs(bb, m):
                act.wait_ge(s_act, bb * NSLICE + KT + m + 1)
                nc.scalar.activation(turn[m], turn[m], ACT.Abs,
                                     bias=minus_quarter[:, :]).then_inc(abs_done, 1)

            def h_sin(bb, m):
                act.wait_ge(abs_done, bb * KT + m + 1)
                nc.scalar.activation(turn[m], turn[m], ACT.Sin, scale=-math.pi,
                                     bias=half_pi[:, :]).then_inc(sin_done, 1)

            def h_high(bb, m):
                act.wait_ge(h_done, bb * KT + m + 1)
                nc.scalar.activation(h_h[:, m, :], turn[m], ACT.Copy).then_inc(hhi, 1)

            def h_all(bb):
                turn_abs(bb, KT - 1)
                for m in range(KT + 1):
                    if m < KT:
                        h_sin(bb, m)
                    if m:
                        h_high(bb, m - 1)

            for s in range(NSLICE):
                if s == KT:
                    act.wait_ge(stage_done, 4 * KT)
                gate(0, s, bank[(s + 4) % 8][:, :])
            h_all(0)
            for st in range(STAGES):
                act.wait_ge(bias_mm, st + 1)
                nc.scalar.activation(bias[:, st, :], bank[4 + st][:, :], ACT.Copy,
                                     accum_out=rowsum[:, 16 + st:17 + st]).then_inc(bias_sum, 1)

            def z_high(b, st, i):
                t = st * NT + i
                act.wait_ge(t_mm, b * 12 + t + 1)
                nc.scalar.activation(z_h[:, :, i * P:(i + 1) * P],
                                     bank[4 + t % 2][:, :].rearrange("p (k t) -> p k t", k=KT),
                                     ACT.Copy).then_inc(zhi, 1)

            def square(b, st, i):
                n = st * NT + i
                if n:
                    act.wait_ge(sq_done, b * 16 + n)
                act.wait_ge(v_done, b * 16 + n + 1 + STAGES)
                nc.scalar.activation(junk[:, :], work[:, i, :], ACT.Square,
                                     accum_out=sumsq[:, n:n + 1]).then_inc(sq_done, 1)

            def batch(b, with_next):
                seq = order(with_next)
                for pos, (kind, one, two) in enumerate(seq):
                    if pos >= LAG and transposed(seq[pos - LAG]):
                        z_high(b, *seq[pos - LAG][1:])
                    if kind == "Y":
                        square(b, one, two)
                        if with_next and (one, two) == (STAGES - 1, 0):
                            h_sin(b + 1, 2)
                            h_high(b + 1, 1)
                            h_sin(b + 1, 3)
                            h_high(b + 1, 2)
                            h_high(b + 1, 3)
                    else:
                        gate(b + 1, one, bank[one % KT][:, :])
                    if with_next:
                        if pos == 0:
                            lora_high(b + 1, 0, lsum)
                        if LORA_AT <= pos < LORA_AT + NSLICE:
                            lora_high(b + 1, pos - LORA_AT + 1, lsum)
                        if pos in X_AT:
                            x_high(b + 1, pos - X_AT[0])
                    if kind == "S" and one == NSLICE - 1:
                        turn_abs(b + 1, KT - 1)
                        h_sin(b + 1, 0)
                        h_sin(b + 1, 1)
                        h_high(b + 1, 0)

            with act.Fori(0, B - 1) as b:
                batch(b, True)
            batch(B - 1, False)

        @block.vector
        def _(dve):
            own = Tally(dve_chain)
            ph, kk = gb[0:4, 0, :], work[0:4, 0, :]

            def fold_low(k):
                dve.wait_ge(hi_done, k + 1)
                nc.vector.tensor_tensor(x_l[:, k, :], amp[:, k, :], x_h[:, k, :].bitcast(F32), ALU.subtract)
                nc.vector.tensor_tensor(mb_l[:, k, :], fold[:, k, :], mb_h[:, k, :].bitcast(F32),
                                        ALU.subtract).then_inc(lo_done, 1)

            for k in range(KT):
                fold_low(k)
            dve.wait_ge(b_hi, 1)
            nc.vector.tensor_tensor(am_l[:, :], b_raw, am_h[:, :].bitcast(F32), ALU.subtract).then_inc(b_lo, 1)

            dve.wait_ge(rows_in, 32)
            own.inc(nc.vector.tensor_scalar(kk, ph, 1.0 / (2 * math.pi), ROUND, ALU.mult, ALU.add), dve)
            own.inc(nc.vector.tensor_scalar(kk, kk, ROUND, None, ALU.subtract), dve)
            for part in TWO_PI:
                own.inc(nc.vector.scalar_tensor_tensor(ph, kk, -part, ph, ALU.mult, ALU.add), dve)
            nc.vector.tensor_scalar(ph, ph, PI_BELOW, -PI_BELOW, ALU.min, ALU.max).then_inc(reduced, 1)

            dve.wait_ge(trig, 2)
            dve.wait_ge(const_done, 5)
            nc.vector.tensor_tensor(mod_rows, work[0:4, 1, :], work[0:4, 0, :], ALU.add).then_inc(rows_done, 1)
            for l in range(L):
                own.inc(nc.vector.tensor_tensor(layer_rows[:, l:l + 1], ident[:, 2 * l:2 * l + 1],
                                                ident[:, 2 * l + 1:2 * l + 2], ALU.add), dve)
            dve.wait_ge(rows_done, 1)
            for l in range(L):
                nc.vector.scalar_tensor_tensor(bias[0:4, 2 * l + 1, :], gb[0:4, 1, :], layer_rows[0:4, l:l + 1],
                                               mod_rows, ALU.mult, ALU.mult).then_inc(rows_done, 1)

            dve.wait_ge(small_in, 32)
            own.inc(nc.vector.tensor_copy(idx_f[:, :], idx_i[:, :]), dve)
            own.inc(nc.vector.tensor_copy(pcol[:, :], pcol_i[:, :]), dve)
            own.inc(nc.vector.tensor_scalar(idx_f[:, :], idx_f[:, :], -float(RANK), pcol[:, :], ALU.mult, ALU.add), dve)
            own.inc(nc.vector.tensor_scalar(tmp4[:, :], idx_f[:, :], 0.0, None, ALU.is_ge), dve)
            own.inc(nc.vector.scalar_tensor_tensor(tmp4[:, :], idx_f[:, :], float(RANK), tmp4[:, :],
                                                   ALU.is_lt, ALU.mult), dve)
            own.inc(nc.vector.tensor_scalar(pick[:, :], tmp4[:, :], col[:, SCALE:SCALE + 1], None, ALU.mult), dve)

            dve.wait_ge(entpb_in, 32)
            dve.wait_ge(rows_done, L + 1)
            nc.vector.memset(negmean[:, :], 0.0).then_inc(acc_done, 1)

            def ent_low(l, k):
                raw2 = raw_slot[at["E", l, k] % RING].rearrange("p (a b) -> p a b", a=2)
                slot, e = k % RING, l * FT + k
                column = col[:, ENT_B + e:ENT_B + e + 1]
                dve.wait_ge(hi_done, KT + e + 1)
                nc.vector.tensor_tensor(ring_l[slot], raw2, ring_h[slot].bitcast(F32),
                                        ALU.subtract).then_inc(lo_done, 1)
                dve.wait_ge(acc_done, e + 1)
                nc.vector.scalar_tensor_tensor(bias[:, 2 * l, :], raw2[:, 1, :], column, bias[:, 2 * l, :],
                                               ALU.mult, ALU.add).then_inc(acc_done, 1)

            def ent_lows(l, first, count=RING):
                for k in range(first, first + count):
                    ent_low(l, k)

            def stage_tile(u, st, k):
                t = tile[u % 2]
                gain, shift = gain_col(st, k), shift_col(st, k)
                dve.wait_ge(summed, u + 1)
                nc.vector.tensor_scalar(negmean[:, u:u + 1], rowsum[:, u:u + 1], -1.0 / D, -1.0 / D,
                                        ALU.mult, ALU.add)
                own.inc(nc.vector.tensor_tensor(t[:, k * P:(k + 1) * P], t[:, k * P:(k + 1) * P],
                                                ident[:, :], ALU.add), dve)
                nc.vector.tensor_scalar(t, t, negmean[:, u:u + 1], None, ALU.add).then_inc(centred, 1)
                if shift is not None:
                    dve.wait_ge(centred, u + 1)
                    own.inc(nc.vector.scalar_tensor_tensor(bias[:, st, :], t, shift, bias[:, st, :],
                                                           ALU.mult, ALU.add), dve)
                dve.wait_ge(stage_hi, u + 1)
                high = stage_h[:, st, k, :].bitcast(F32)
                if gain is None:
                    low = nc.vector.tensor_tensor(stage_l[:, st, k, :], t, high, ALU.subtract)
                else:
                    low = nc.vector.scalar_tensor_tensor(stage_l[:, st, k, :], t, gain, high,
                                                         ALU.mult, ALU.subtract)
                low.then_inc(stage_done, 1)

            def lora_sum(bb, c, place, source):
                if c == 0:
                    nc.vector.tensor_scalar(place[0], a_all[:, :], pick[:, bass.ds(bb, 1)], None,
                                            ALU.mult).then_inc(lsum_done, 1)
                else:
                    h, k = divmod(c - 1, KT)
                    if c >= 2:
                        dve.wait_ge(llo, bb * ITEMS + c - 1)
                    dve.wait_ge(l_mm, bb * NSLICE + c)
                    nc.vector.tensor_tensor(place[c % 2], source, fold[:, k, h * D:(h + 1) * D],
                                            ALU.add).then_inc(lsum_done, 1)

            def lora_low(bb, c, place):
                dve.wait_ge(lhi, bb * ITEMS + c + 1)
                if c == 0:
                    low, high = am_l[:, :], am_h[:, :]
                else:
                    h, k = divmod(c - 1, KT)
                    low, high = mb_l[:, k, h * D:(h + 1) * D], mb_h[:, k, h * D:(h + 1) * D]
                nc.vector.tensor_tensor(low, place[c % 2], high.bitcast(F32), ALU.subtract).then_inc(llo, 1)

            def x_low(bb, half):
                s = slice(2 * half, 2 * half + 2)
                dve.wait_ge(xhi, bb * 2 + half + 1)
                nc.vector.tensor_tensor(x_l[:, s, :], amp[:, s, :], x_h[:, s, :].bitcast(F32),
                                        ALU.subtract).then_inc(xlo, 1)

            ent_lows(0, 0)
            dve.wait_ge(step_done, KT)
            for m in range(KT):
                nc.vector.tensor_copy(fold[:, m, D:2 * D], bank[KT + m][:, :]).then_inc(m_dve, 1)
            dve.wait_ge(a_in, 16)
            lora_sum(0, 0, lsum_first, None)
            for h in range(2):
                dve.wait_ge(q_hi, h + 1)
                nc.vector.tensor_tensor(q_l[:, h * D:(h + 1) * D], bank[h][:, :],
                                        q_h[:, h * D:(h + 1) * D].bitcast(F32), ALU.subtract).then_inc(q_lo, 1)
            lora_low(0, 0, lsum_first)
            dve.wait_ge(m_act, KT)
            for j in range(RING):
                for c in (2 * j + 1, 2 * j + 2):
                    lora_sum(0, c, lsum_first, bank[2 + (c - 1) % 2][:, :])
                for c in (2 * j + 1, 2 * j + 2):
                    lora_low(0, c, lsum_first)
                ent_lows(0, RING + j, 1)
            x_low(0, 0)
            x_low(0, 1)
            for l in range(L):
                if l:
                    ent_lows(l, 0)
                    for k in range(KT):
                        stage_tile(ENT_U[l - 1] + k, 2 * (l - 1), k)
                    ent_lows(l, RING)
                for k in range(KT):
                    ent_lows(l, 2 * RING + k, 1)
                    stage_tile(PATH_U[l] + k, 2 * l + 1, k)
                ent_lows(l, 3 * RING)
            for k in range(KT):
                stage_tile(ENT_U[L - 1] + k, 2 * (L - 1), k)

            def h_product(bb, m):
                dve.wait_ge(sin_done, bb * KT + m + 1)
                nc.vector.scalar_tensor_tensor(turn[m], turn[m], math.sqrt(2), amp[:, m, :],
                                               ALU.mult, ALU.mult).then_inc(h_done, 1)

            def h_low(bb, m):
                dve.wait_ge(hhi, bb * KT + m + 1)
                nc.vector.tensor_tensor(h_l[:, m, :], turn[m], h_h[:, m, :].bitcast(F32),
                                        ALU.subtract).then_inc(hlo, 1)

            for m in range(KT + 1):
                if m < KT:
                    h_product(0, m)
                if m:
                    h_low(0, m - 1)
            for st in range(STAGES):
                dve.wait_ge(bias_sum, st + 1)
                c = slice(16 + st, 17 + st)
                own.inc(nc.vector.tensor_scalar(negmean[:, c], rowsum[:, c], -1.0 / D, None, ALU.mult), dve)
                nc.vector.tensor_scalar(bias[:, st, :], bias[:, st, :], negmean[:, c], None,
                                        ALU.add).then_inc(v_done, 1)
            dve.wait_ge(v_done, STAGES)

            def stage_out(b, st, i):
                n = st * NT + i
                dve.wait_ge(y_mm, b * 16 + n + 1)
                if st == 0:
                    nc.vector.tensor_tensor(work[:, i, :], bank[i][:, :], bias[:, st, :],
                                            ALU.add).then_inc(v_done, 1)
                else:
                    dve.wait_ge(r_done, b * 8 + (n - NT) // 2 + 1)
                    nc.vector.scalar_tensor_tensor(work[:, i, :], bank[i][:, :], rstd[:, n - NT:n - NT + 1],
                                                   bias[:, st, :], ALU.mult, ALU.add).then_inc(v_done, 1)

            def z_low(b, st, i):
                t = st * NT + i
                dve.wait_ge(zhi, b * 12 + t + 1)
                nc.vector.tensor_tensor(z_l[:, :, i * P:(i + 1) * P],
                                        bank[4 + t % 2][:, :].rearrange("p (k t) -> p k t", k=KT),
                                        z_h[:, :, i * P:(i + 1) * P].bitcast(F32), ALU.subtract).then_inc(zlo, 1)

            def finish(b, i):
                n = (STAGES - 1) * NT + i
                dve.wait_ge(r_done, b * 8 + n // 2 + 1)
                own.inc(nc.vector.scalar_tensor_tensor(work[:, i, :], work[:, i, :], rstd[:, n:n + 1], gb[:, 0, :],
                                                       ALU.mult, ALU.mult), dve)
                dve.wait_ge(res_done, b * NT + i + 1)
                nc.vector.tensor_tensor(res[:, i, :], work[:, i, :], res[:, i, :], ALU.add).then_inc(out_done, 1)

            def batch(b, with_next):
                seq = order(with_next)
                for pos, (kind, one, two) in enumerate(seq):
                    if kind == "Y":
                        if with_next and (one, two) == (STAGES - 1, 1):
                            h_product(b + 1, 2)
                            h_low(b + 1, 1)
                        stage_out(b, one, two)
                        if with_next and (one, two) == (STAGES - 1, 0):
                            h_product(b + 1, 0)
                            h_product(b + 1, 1)
                            h_low(b + 1, 0)
                        if with_next and (one, two) == (STAGES - 1, 1):
                            h_product(b + 1, 3)
                            h_low(b + 1, 2)
                            h_low(b + 1, 3)
                    if pos >= LAG and transposed(seq[pos - LAG]):
                        z_low(b, *seq[pos - LAG][1:])
                    if with_next:
                        c = 0 if pos == 0 else pos - LORA_AT + 1
                        if pos == 0 or LORA_AT <= pos < LORA_AT + NSLICE:
                            lora_sum(b + 1, c, lsum, bank[6 + (c - 1) % 2][:, :])
                            lora_low(b + 1, c, lsum)
                        if pos in X_AT:
                            x_low(b + 1, pos - X_AT[0])
                for i in range(NT):
                    finish(b, i)

            with dve.Fori(0, B - 1) as b:
                own.enter(b * NT)
                batch(b, True)
            own.leave(B - 1)
            batch(B - 1, False)

        @block.tensor
        def _(pe):
            def split_product(dst, parts):
                passes = [(a, b) for lh, ll, rh, rl in parts for a, b in ((lh, rh), (lh, rl), (ll, rh))]
                for n, (a, b) in enumerate(passes):
                    last = nc.tensor.matmul(dst, a, b, start=n == 0, stop=n == len(passes) - 1)
                return last

            def fold_step(slot_h, slot_l, rhs_h, rhs_l, banks, first, final):
                for m in range(KT):
                    s = slice(m * P, (m + 1) * P)
                    for q, bk in enumerate(banks[m]):
                        c = slice(q * D, (q + 1) * D)
                        passes = ((slot_h[:, s], rhs_h[:, c]), (slot_h[:, s], rhs_l[:, c]), (slot_l[:, s], rhs_h[:, c]))
                        for n, (a, b) in enumerate(passes):
                            last = nc.tensor.matmul(bank[bk][:, :], a, b, start=first and n == 0,
                                                    stop=final and n == 2)
                last.then_inc(step_done, 1)

            for k in range(KT):
                pe.wait_ge(lo_done, k + 1)
                fold_step(x_h[:, k, :], x_l[:, k, :], mb_h[:, k, :], mb_l[:, k, :],
                          [(m, KT + m) for m in range(KT)], k == 0, k == KT - 1)
            pe.wait_ge(b_lo, 1)
            for h in range(2):
                pe.wait_ge(m_act, h + 1)
                c = slice(h * D, (h + 1) * D)
                split_product(bank[h][:, :], [
                    (am_h[:, k * P:(k + 1) * P], am_l[:, k * P:(k + 1) * P], mb_h[:, k, c], mb_l[:, k, c])
                    for k in range(KT)]).then_inc(q_mm, 1)

            def spread_mod(l, first_bank):
                for p in range(2):
                    row = 2 * l + p
                    last = nc.tensor.matmul(bank[first_bank + p][:, :], ident[0:4, row:row + 1].to_broadcast([4, P]),
                                            mod_rows, start=True, stop=True)
                last.then_inc(mod_mm, 1)

            def ent_step(l, j, value, first, final):
                pe.wait_ge(lo_done, value)
                fold_step(ring_h[j][:, 0, :], ring_l[j][:, 0, :], ring_h[j][:, 1, :], ring_l[j][:, 1, :],
                          [(fold_bank(l, m),) for m in range(KT)], first, final)

            def ent_rest(l):
                with pe.Fori(0, FT // RING - 2) as i:
                    for j in range(RING):
                        ent_step(l, j, KT + l * FT + RING + j + 1 + i * RING, False, False)
                for j in range(RING):
                    ent_step(l, j, KT + (l + 1) * FT - RING + j + 1, False, j == RING - 1)

            def lora_product(bb, c, dst):
                h, k = divmod(c - 1, KT)
                s, q = slice(k * P, (k + 1) * P), slice(h * D, (h + 1) * D)
                split_product(dst, [(am_h[:, s], am_l[:, s], q_h[:, q], q_l[:, q])]).then_inc(l_mm, 1)

            pe.wait_ge(rows_done, 1)
            pe.wait_ge(m_act, KT)
            spread_mod(0, 2)
            pe.wait_ge(m_dve, KT)
            for j in range(RING):
                ent_step(0, j, KT + j + 1, j == 0, False)
                for c in (2 * j + 1, 2 * j + 2):
                    if c == 1:
                        pe.wait_ge(llo, 1)
                        pe.wait_ge(q_lo, 2)
                        pe.wait_ge(mod_in, 2)
                    if c > 2:
                        pe.wait_ge(lsum_done, c - 1)
                    lora_product(0, c, bank[2 + (c - 1) % 2][:, :])
            spread_mod(1, 0)
            ent_rest(0)
            pe.wait_ge(mod_in, 4)
            pe.wait_ge(lsum_done, ITEMS)
            for j in range(RING):
                ent_step(1, j, KT + FT + j + 1, j == 0, False)
            ent_rest(1)

            def slice_product(bb, s, dst):
                h, m = divmod(s, KT)
                c = slice(h * D + m * P, h * D + (m + 1) * P)
                if s == 0:
                    pe.wait_ge(xlo, bb * 2 + 2)
                    pe.wait_ge(llo, bb * ITEMS + 1 + KT)
                if s == KT:
                    pe.wait_ge(llo, bb * ITEMS + ITEMS)
                split_product(dst, [(mb_h[:, k, c], mb_l[:, k, c], x_h[:, k, :], x_l[:, k, :])
                                    for k in range(KT)]).then_inc(s_mm, 1)

            pe.wait_ge(summed, ENT_U[0] + KT)
            for s in range(NSLICE):
                if s == KT:
                    pe.wait_ge(summed, ENT_U[1] + KT)
                slice_product(0, s, bank[(s + 4) % 8][:, :])
            pe.wait_ge(stage_done, 16)
            pe.wait_ge(s_act, KT)
            for st in range(STAGES):
                nc.tensor.matmul(bank[4 + st][:, :], ones[:, :], bias[:, st, :], start=True,
                                 stop=True).then_inc(bias_mm, 1)

            def stage_product(b, st, i, with_next):
                n = st * NT + i
                s = slice(i * P, (i + 1) * P)
                if st == 0:
                    if i == 0:
                        pe.wait_ge(s_act, b * NSLICE + NSLICE)
                        pe.wait_ge(hlo, b * KT + KT)
                    src_h, src_l = h_h, h_l
                else:
                    pe.wait_ge(zlo, b * 12 + n - NT + 1)
                    src_h, src_l = z_h, z_l
                pe.wait_ge(v_done, b * 16 + n + 1)
                if st == STAGES - 1 and with_next:
                    pe.wait_ge(s_act, b * NSLICE + NSLICE + KT + i + 1)
                split_product(bank[i][:, :], [(src_h[:, k, s], src_l[:, k, s], stage_h[:, st, k, :],
                                               stage_l[:, st, k, :]) for k in range(KT)]).then_inc(y_mm, 1)

            def transpose_tile(b, st, i):
                t = st * NT + i
                pe.wait_ge(v_done, b * 16 + t + 1 + STAGES)
                if t >= 2:
                    pe.wait_ge(zlo, b * 12 + t - 1)
                for k in range(KT):
                    last = nc.tensor.transpose(bank[4 + t % 2][:, k * P:(k + 1) * P], work[:, i, k * P:(k + 1) * P],
                                               ident[:, :])
                last.then_inc(t_mm, 1)

            def batch(b, with_next):
                seq = order(with_next)
                for pos, (kind, one, two) in enumerate(seq):
                    if kind == "Y":
                        stage_product(b, one, two, with_next)
                    else:
                        if one < KT:
                            pe.wait_ge(v_done, b * 16 + 2 * NT + one + 1 + STAGES)
                        else:
                            pe.wait_ge(s_act, b * NSLICE + NSLICE + one - KT + 1)
                        slice_product(b + 1, one, bank[one % KT][:, :])
                    if pos >= LAG and transposed(seq[pos - LAG]):
                        transpose_tile(b, *seq[pos - LAG][1:])
                    if with_next and LORA_AT <= pos < LORA_AT + NSLICE:
                        c = pos - LORA_AT + 1
                        pe.wait_ge(llo, (b + 1) * ITEMS + 1)
                        if c > 2:
                            pe.wait_ge(lsum_done, (b + 1) * ITEMS + c - 1)
                        lora_product(b + 1, c, bank[6 + (c - 1) % 2][:, :])

            with pe.Fori(0, B - 1) as b:
                batch(b, True)
            batch(B - 1, False)


def kernel(**inputs):
    import numpy as np
    import concourse.bacc as bacc
    from concourse.bass_utils import run_bass_kernel_spmd

    def a(name):
        return np.asarray(inputs[name])

    def columns(v, tiles):
        return v.reshape(-1, tiles, P).transpose(2, 0, 1).reshape(P, -1)

    f = lambda name: a("L0_ffn_" + name)
    x = a("x")
    tokens = x.reshape(B, P, NT, D)
    arrays = {
        "xt": tokens.reshape(B, P, NT, KT, P).transpose(0, 4, 3, 2, 1).reshape(B, P, KT, T),
        "xr": tokens,
        "wc": a("L0_cond_W").reshape(KT, P, D),
        "ap": np.concatenate([f("amp_w"), f("ph_w")], axis=1).reshape(KT, P, 2 * D),
        "bt": a("L0_cond_Bm").reshape(NADAPT, KT, P, RANK).transpose(2, 1, 0, 3).reshape(P, KT * NADAPT * RANK),
        "aa": a("L0_cond_A").reshape(NADAPT * RANK, D),
        "idx": a("itok_B_0_6"),
        "cols": np.concatenate([
            columns(f("amp_b"), KT), columns(f("ph_b"), KT), columns(f("ent_b"), FT),
            columns(f("ln3_g"), KT), columns(f("ln3_b"), KT), columns(f("ln4_g"), KT), columns(f("ln4_b"), KT),
            np.repeat(a("L0_cond_scalings"), RANK).reshape(P, 1)], axis=1),
        "phase": f("phase").reshape(L * 2, D),
        "pathb": f("path_b").reshape(L * 2, D),
        "entpb": f("ent_pb"),
        "gb_rows": np.stack([f("ln4_g")[L - 1], f("ln4_b")[L - 1]]),
        "ent": np.concatenate([f("ent_w").transpose(0, 2, 1), f("ent_pw")], axis=2).reshape(L, FT, P, 2 * D),
        "path": f("path_w").reshape(L, 2, KT, P, D).transpose(0, 2, 3, 1, 4).reshape(L, KT, P, 2 * D),
    }
    nc = bacc.Bacc("TRN2", target_bir_lowering=False, num_devices=1, dynamic_dma_scratch_size=1024)
    sent, args = {}, []
    for name, v in arrays.items():
        v = np.ascontiguousarray(v)
        sent["in_" + name] = v
        args.append(nc.dram_tensor("in_" + name, v.shape, mybir.dt.from_np(v.dtype), kind="ExternalInput").ap())
    out = nc.dram_tensor("out_0", (B, P, NT, D), F32, kind="ExternalOutput").ap()
    build(nc, *args, out)
    r = run_bass_kernel_spmd(nc, [sent], core_ids=[0])
    return r.results[0]["out_0"].reshape(B, T, D)
```

```python
import concourse.bass as bass
from concourse import mybir
from contextlib import ExitStack
import math

F32 = mybir.dt.float32
F32R = mybir.dt.float32r
I32 = mybir.dt.int32
ACT = mybir.ActivationFunctionType
ALU = mybir.AluOpType

P = 128
D = 512
B = 4
T = 512
KT = D // P
NT = T // P
L = 2
F = 2048
FT = F // P
NADAPT, RANK = 8, 16
EPS = 1e-5
STAGES = 2 * L
RING = 4
PATH_LOAD = ((6, 9, 11, 13), (3, 6, 8, 11))
PATH_TILE = ((8, 11, 13, 15), (5, 7, 10, 13))
NSLICE = 8

AMP_B, PH_B = 0, KT
ENT_B = 2 * KT
LN3_G = ENT_B + L * FT
LN3_B = LN3_G + L * KT
LN4_G = LN3_B + L * KT
LN4_B = LN4_G + L * KT
SCALE = LN4_B + L * KT
NCOLS = SCALE + 1


ROUND = 1.5 * 2 ** 23
TWO_PI = [6.28125, round((2 * math.pi - 6.28125) * 2 ** 20) / 2 ** 20]
TWO_PI.append(2 * math.pi - sum(TWO_PI))
PI_BELOW = 3.1415925


class Tally:

    def __init__(self, sem):
        self.sem, self.count, self.loop = sem, 0, 0

    def enter(self, loop):
        self.loop, self.start = loop, self.count

    def leave(self, iterations):
        self.loop, self.count = 0, self.start + iterations * (self.count - self.start)

    def inc(self, instruction, engine=None):
        self.count += 1
        instruction.then_inc(self.sem, 1)
        if engine is not None:
            engine.wait_ge(self.sem, self.loop + self.count)


def build(nc, xt, xr, wc, ap, bt, aa, idx, cols, phase, pathb, entpb, gb_rows, ent, path, out):
    ctx = ExitStack()
    with ctx:
        def sb(name, shape, dt=F32):
            return ctx.enter_context(nc.sbuf_tensor(name, shape, dt))

        def sem(name):
            return ctx.enter_context(nc.semaphore(name))

        stage_h = sb("stage_h", [P, STAGES, KT, D], F32R)
        stage_l = sb("stage_l", [P, STAGES, KT, D], F32R)
        fold = sb("fold", [P, KT, 2 * D])
        q_h = sb("q_h", [P, 2 * D], F32R)
        q_l = sb("q_l", [P, 2 * D], F32R)
        bias = sb("bias", [P, STAGES, D])
        gb = sb("gb", [P, 2, D])
        a_stack = sb("a_stack", [P, D], F32R)
        q_stack = sb("q_stack", [P, D], F32R)
        select = sb("select", [P, 7 * RANK], F32R)
        target = sb("target", [P, 7 * RANK])
        col = sb("col", [P, NCOLS])
        ident = sb("ident", [P, P])
        mb_h = sb("mb_h", [P, KT, 2 * D], F32R)
        mb_l = sb("mb_l", [P, KT, 2 * D], F32R)
        x_h = sb("x_h", [P, KT, T], F32R)
        x_l = sb("x_l", [P, KT, T], F32R)
        am_h = sb("am_h", [P, D], F32R)
        am_l = sb("am_l", [P, D], F32R)
        h_h = sb("h_h", [P, KT, T], F32R)
        h_l = sb("h_l", [P, KT, T], F32R)
        z_h = sb("z_h", [P, KT, T], F32R)
        z_l = sb("z_l", [P, KT, T], F32R)
        amp = sb("amp", [P, KT, T])
        work = sb("work", [P, NT, D])
        mod = sb("mod", [P, 2, D])
        raw = sb("raw", [P, 3, 2 * D])
        idx_i = sb("idx_i", [P, B], I32)
        idx_f = sb("idx_f", [P, B])
        target_i = sb("target_i", [P, RANK], I32)
        rowsum = sb("rowsum", [P, 16 + STAGES])
        negmean = sb("negmean", [P, 16 + STAGES])
        layer_rows = sb("layer_rows", [P, L])
        unread = sb("unread", [P, 1])
        half_pi = sb("half_pi", [P, 1])
        minus_quarter = sb("minus_quarter", [P, 1])
        sumsq = sb("sumsq", [P, 16])
        var = sb("var", [P, 16])
        minus_half = sb("minus_half", [P, 2])
        eps_sum = sb("eps_sum", [P, 2])
        newton_a = sb("newton_a", [P, 2])
        newton_b = sb("newton_b", [P, 2])
        root = sb("root", [P, 16])
        corr = sb("corr", [P, 16])
        rstd = sb("rstd", [P, 16])

        bank = [ctx.enter_context(nc.psum_tensor(f"bank{i}", [P, 512], F32)) for i in range(8)]

        raw_slot = [raw[:, 0, :], raw[:, 1, :], raw[:, 2, :],
                    work[:, 0:2, :].rearrange("p a b -> p (a b)")]
        ring_h = [h_h[:, 0:2, :], h_h[:, 2:4, :], z_h[:, 0:2, :], z_h[:, 2:4, :]]
        ring_l = [h_l[:, 0:2, :], h_l[:, 2:4, :], z_l[:, 0:2, :], z_l[:, 2:4, :]]
        tile = [work[:, 2, :], work[:, 3, :]]
        b_raw, a_raw = work[:, 2, :], work[:, 3, :]
        ones = work[:, 0, 0:P]
        lsum = [raw[:, 2, 0:D], raw[:, 2, D:2 * D]]
        turn = [mod[:, 0, :], mod[:, 1, :], lsum[0], lsum[1]]
        gates = [amp[:, m, :] for m in range(KT)]
        res = raw[:, 0:2, :].rearrange("p a (b c) -> p (a b) c", b=2)
        lsum_first = tile
        mod_rows = gb[0:4, 0, :]
        pick_q_low, pick_a_low, pick_a_high, pick_q_high = [
            select[:, u * RANK:(u + 3) * RANK] for u in (0, 1, 2, 4)]
        STACK = [slice(0, 3 * RANK), slice(64, 64 + 3 * RANK)]

        w_in = [sem(f"w_in{k}") for k in range(KT)]
        amp_in = [sem(f"amp_in{k}") for k in range(KT)]
        ph_in = [sem(f"ph_in{k}") for k in range(KT)]
        small_in = sem("small_in")
        rows_in = sem("rows_in")
        entpb_in = sem("entpb_in")
        b_in = sem("b_in")
        a_in = sem("a_in")
        gb_in = sem("gb_in")
        raw_in = [sem(f"raw_in{s}") for s in range(RING)]
        x_in = sem("x_in")
        res_in = sem("res_in")
        stored = [sem(f"stored{i}") for i in range(NT)]
        const_done = sem("const_done")
        pool_chain = sem("pool_chain")
        dve_chain = sem("dve_chain")
        act_chain = sem("act_chain")
        reduced = sem("reduced")
        trig = sem("trig")
        rows_done = sem("rows_done")
        hi_done = sem("hi_done")
        lo_done = sem("lo_done")
        step_done = sem("step_done")
        acc_done = sem("acc_done")
        b_hi = sem("b_hi")
        b_lo = sem("b_lo")
        m_mm = sem("m_mm")
        m_act = sem("m_act")
        m_dve = sem("m_dve")
        q_mm = sem("q_mm")
        q_hi = sem("q_hi")
        q_lo = sem("q_lo")
        mod_mm = sem("mod_mm")
        mod_in = sem("mod_in")
        scaled = sem("scaled")
        summed = sem("summed")
        mean_done = sem("mean_done")
        centred = sem("centred")
        stage_hi = sem("stage_hi")
        stage_done = sem("stage_done")
        ones_done = sem("ones_done")
        bias_mm = sem("bias_mm")
        bias_sum = sem("bias_sum")
        bias_done = sem("bias_done")
        y_mm = sem("y_mm")
        s_mm = sem("s_mm")
        l_mm = sem("l_mm")
        t_mm = sem("t_mm")
        v_done = sem("v_done")
        sq_done = sem("sq_done")
        r_done = sem("r_done")
        zhi = sem("zhi")
        zlo = sem("zlo")
        scaled_a = sem("scaled_a")
        a_split = sem("a_split")
        select_done = sem("select_done")
        a_mm = sem("a_mm")
        q_sel_mm = sem("q_sel_mm")
        a_stacked = sem("a_stacked")
        q_stacked = sem("q_stacked")
        lsum_done = sem("lsum_done")
        lhi = sem("lhi")
        llo = sem("llo")
        xhi = sem("xhi")
        xlo = sem("xlo")
        s_act = sem("s_act")
        abs_done = sem("abs_done")
        sin_done = sem("sin_done")
        h_done = sem("h_done")
        hhi = sem("hhi")
        hlo = sem("hlo")
        res_done = sem("res_done")
        gained = sem("gained")
        out_done = sem("out_done")

        STEPS = []
        for l in range(L):
            for k in range(FT):
                if k in PATH_LOAD[l]:
                    STEPS.append(("P", l, PATH_LOAD[l].index(k)))
                STEPS.append(("E", l, k))
        at = {step: g for g, step in enumerate(STEPS)}

        def raw_value(g):
            return 16 * (g // RING + 1)

        def slice_columns(s):
            h, m = divmod(s, KT)
            return slice((1 - h) * D + m * P, (1 - h) * D + (m + 1) * P)

        def lora_tile(c):
            h, k = divmod(c - 1, KT)
            return k, slice((1 - h) * D, (2 - h) * D)

        def first_bank(c):
            return (c + 2) % 4 if c <= KT else (c - 1) % 2

        def stack_rows(c):
            return STACK[(c - 1) // KT]

        def gain_col(st, k):
            if st == 0:
                return None
            base = LN3_G + (st // 2) * KT if st % 2 else LN4_G
            return col[:, base + k:base + k + 1]

        def shift_col(st, k):
            if st == 0:
                return None
            base = LN3_B + (st // 2) * KT if st % 2 else LN4_B
            return col[:, base + k:base + k + 1]

        PATH_U = [2 * l * KT for l in range(L)]
        ENT_U = [(2 * l + 1) * KT for l in range(L)]
        LO_FOLD = 3 * KT
        LORA_EARLY = {1: (1, 2), 2: (3, 4)}
        LORA_LATE = {12: (5, 6), 13: (7, 8)}
        X_FIRST = (8, 9, 10, 11)
        BIAS_ORDER = (0, 1, 3, 2)
        WARM = 11
        ITEMS = NSLICE

        def order(with_next):
            y = [("Y", st, i) for st in range(STAGES) for i in range(NT)]
            s = [("S", s, 0) for s in range(NSLICE)] if with_next else []
            return y[:12] + s + y[12:]

        LAG = 2
        SELECT_AT = 2
        LORA_AT = 5
        X_AT = (1, 2, 3, 4)

        def transposed(item):
            return item[0] == "Y" and item[1] < STAGES - 1

        block = ctx.enter_context(nc.Block())

        @block.sync
        def _(sp):
            for k in range(KT):
                sp.dma_start(amp[:, k, :], wc[k]).then_inc(w_in[k], 16)
                sp.dma_start(fold[:, k, 0:D], ap[k, :, 0:D]).then_inc(amp_in[k], 16)
                sp.dma_start(fold[:, k, D:2 * D], ap[k, :, D:2 * D]).then_inc(ph_in[k], 16)
            sp.dma_start(gb[0:4, 0, :], phase).then_inc(rows_in, 16)
            sp.dma_start(gb[0:4, 1, :], pathb).then_inc(rows_in, 16)
            sp.dma_start(col[:, :], cols).then_inc(small_in, 16)
            sp.dma_start(idx_i[:, :], idx.partition_broadcast(P)).then_inc(small_in, 16)
            sp.dma_start(b_raw, bt).then_inc(b_in, 16)
            sp.dma_start(a_raw, aa).then_inc(a_in, 16)
            for g, (kind, l, k) in enumerate(STEPS):
                if g == RING - 1:
                    sp.wait_ge(rows_done, L + 1)
                if g >= RING:
                    was, wl, wk = STEPS[g - RING]
                    if was == "E":
                        sp.wait_ge(acc_done, wl * FT + wk + 1)
                    else:
                        sp.wait_ge(scaled, wl * KT + wk + 1)
                sp.dma_start(raw_slot[g % RING], (ent if kind == "E" else path)[l, k]).then_inc(
                    raw_in[g % RING], 16)
                if g == 1:
                    sp.wait_ge(const_done, 2)
                    for layer in range(L):
                        sp.dma_start(bias[0:1, 2 * layer, :], entpb[layer:layer + 1, :]).then_inc(entpb_in, 16)
                if g == RING:
                    sp.wait_ge(lo_done, LO_FOLD)
                    sp.dma_start(amp[:, :, :], xt[0]).then_inc(x_in, 16)

            def batch(b, with_next):
                for i in range(NT):
                    sp.wait_ge(out_done, b * NT + i + 1 + NT)
                    sp.dma_start(out[bass.ds(b, 1)].rearrange("a p t d -> (a p) t d")[:, i, :],
                                 res[:, i, :]).then_inc(stored[i], 16)
                if with_next:
                    for i in range(NT):
                        sp.wait_ge(stored[i], b * 16 + 16)
                    sp.dma_start(res, xr[bass.ds(b + 1, 1)].rearrange(
                        "a p t d -> (a p) t d")).then_inc(res_in, 16)

            sp.wait_ge(mod_mm, 2)
            sp.dma_start(gb[:, :, :], gb_rows.partition_broadcast(P)).then_inc(gb_in, 16)
            sp.wait_ge(acc_done, L * FT)
            sp.dma_start(res, xr[0]).then_inc(res_in, 16)
            with sp.Fori(0, B - 1) as b:
                batch(b, True)
            batch(B - 1, False)
            for i in range(NT):
                sp.wait_ge(stored[i], B * 16)

        @block.gpsimd
        def _(pool):
            own = Tally(pool_chain)
            own.inc(nc.gpsimd.memset(ident[:, :], 0.0), pool)
            nc.gpsimd.affine_select(out=ident[:, :], in_=ident[:, :], compare_op=ALU.not_equal, fill=1.0,
                                    base=0, pattern=[[-1, P]], channel_multiplier=1).then_inc(const_done, 1)
            nc.gpsimd.memset(bias[:, :, :], 0.0).then_inc(const_done, 1)
            nc.gpsimd.memset(half_pi[:, :], math.pi / 2).then_inc(const_done, 1)
            own.inc(nc.gpsimd.memset(minus_quarter[:, :], -0.25), pool)
            nc.gpsimd.iota(target_i[:, :], [[-1, RANK]], base=0, channel_multiplier=1).then_inc(const_done, 1)
            nc.gpsimd.memset(target[:, :], -1000.0).then_inc(const_done, 1)
            own.inc(nc.gpsimd.memset(minus_half[:, :], -0.5), pool)
            own.inc(nc.gpsimd.memset(eps_sum[:, :], D * EPS), pool)
            own.inc(nc.gpsimd.memset(newton_a[:, :], -0.5 * math.sqrt(D)), pool)
            own.inc(nc.gpsimd.memset(newton_b[:, :], 1.5 * math.sqrt(D)), pool)
            nc.gpsimd.memset(corr[:, :], 0.0).then_inc(out_done, NT)
            nc.gpsimd.memset(root[:, :], 0.0).then_inc(v_done, NT)

            for l in range(L):
                pool.wait_ge(mod_in, 2 * (l + 1))
                for k in range(KT):
                    u = PATH_U[l] + k
                    g = at["P", l, k]
                    slot = raw_slot[g % RING].rearrange("p (a b) -> p a b", a=2)
                    pool.wait_ge(raw_in[g % RING], raw_value(g))
                    own.inc(nc.gpsimd.tensor_tensor(slot, slot, mod[:, :, :], ALU.mult), pool)
                    if u >= 2:
                        pool.wait_ge(stage_done, u - 1)
                    elif u == 0:
                        pool.wait_ge(llo, KT)
                    own.inc(nc.gpsimd.tensor_tensor(tile[u % 2], slot[:, 0, :], slot[:, 1, :], ALU.add), pool)
                    diagonal = tile[u % 2][:, k * P:(k + 1) * P]
                    nc.gpsimd.tensor_tensor(diagonal, diagonal, ident[:, :], ALU.add).then_inc(scaled, 1)

            pool.wait_ge(acc_done, L * FT)
            nc.gpsimd.memset(ones, 1.0).then_inc(ones_done, 1)

            def token_scale(b, st, i, tiles=2):
                n = st * NT + i
                c, one = slice(n, n + tiles), slice(0, tiles)
                pool.wait_ge(sq_done, b * 16 + n + tiles)
                own.inc(nc.gpsimd.tensor_tensor(var[:, c], sumsq[:, c], eps_sum[:, one], ALU.add), pool)
                own.inc(nc.gpsimd.tensor_tensor(corr[:, c], var[:, c], newton_a[:, one], ALU.mult))
                own.inc(nc.gpsimd.tensor_tensor(root[:, c], var[:, c], minus_half[:, one], ALU.pow), pool)
                own.inc(nc.gpsimd.tensor_tensor(var[:, c], root[:, c], root[:, c], ALU.mult), pool)
                own.inc(nc.gpsimd.tensor_tensor(var[:, c], var[:, c], corr[:, c], ALU.mult), pool)
                own.inc(nc.gpsimd.tensor_tensor(var[:, c], var[:, c], newton_b[:, one], ALU.add), pool)
                nc.gpsimd.tensor_tensor(rstd[:, c], root[:, c], var[:, c], ALU.mult).then_inc(r_done, 1)

            pool.wait_ge(gb_in, 16)
            links = 6 * STAGES * NT // 2

            def batch(b, with_next):
                for st in range(STAGES):
                    token_scale(b, st, 0)
                    if with_next or st < STAGES - 1:
                        token_scale(b, st, 2)
                    else:
                        token_scale(b, st, 2, 1)
                        token_scale(b, st, 3, 1)
                    if st == 0:
                        pool.wait_ge(res_in, b * 16 + 16)
                        for i in range(NT):
                            nc.gpsimd.tensor_tensor(res[:, i, :], res[:, i, :], gb[:, 1, :],
                                                    ALU.add).then_inc(res_done, 1)
                if with_next:
                    for i in range(NT):
                        pool.wait_ge(gained, b * NT + i + 1)
                        nc.gpsimd.tensor_tensor(res[:, i, :], work[:, i, :], res[:, i, :],
                                                ALU.add).then_inc(out_done, 1)

            with pool.Fori(0, B - 1) as b:
                own.enter(b * links)
                batch(b, True)
            own.leave(B - 1)
            batch(B - 1, False)

        @block.scalar
        def _(act):
            for k in range(KT):
                act.wait_ge(w_in[k], 16)
                nc.scalar.activation(x_h[:, k, :], amp[:, k, :], ACT.Copy).then_inc(hi_done, 1)
                for landed, c in ((amp_in[k], slice(0, D)), (ph_in[k], slice(D, 2 * D))):
                    act.wait_ge(landed, 16)
                    nc.scalar.activation(mb_h[:, k, c], fold[:, k, c], ACT.Copy).then_inc(hi_done, 1)
            act.wait_ge(b_in, 16)
            nc.scalar.activation(am_h[:, :], b_raw, ACT.Copy).then_inc(b_hi, 1)

            act.wait_ge(reduced, 1)
            nc.scalar.activation(work[0:4, 1, :], gb[0:4, 0, :], ACT.Sin).then_inc(trig, 1)
            nc.scalar.activation(work[0:4, 0, :], gb[0:4, 0, :], ACT.Abs).then_inc(act_chain, 1)
            act.wait_ge(act_chain, 1)
            act.wait_ge(const_done, 3)
            nc.scalar.activation(work[0:4, 0, :], work[0:4, 0, :], ACT.Sin, scale=-1.0,
                                 bias=half_pi[0:4, :]).then_inc(trig, 1)

            def ent_high(slot, e, source, landed):
                act.wait_ge(raw_in[source], landed)
                if e >= RING:
                    act.wait_ge(step_done, e - RING + 1)
                nc.scalar.activation(ring_h[slot], raw_slot[source].rearrange("p (a b) -> p a b", a=2),
                                     ACT.Copy).then_inc(hi_done, 1)

            def ent_split(l, k):
                g = at["E", l, k]
                ent_high(k % RING, l * FT + k, g % RING, raw_value(g))

            def stage_sum(u, source):
                nc.scalar.activation(tile[u % 2], source, ACT.Copy,
                                     accum_out=rowsum[:, u:u + 1]).then_inc(summed, 1)

            def stage_high(u, st, k):
                gain, mean = gain_col(st, k), negmean[:, u:u + 1]
                act.wait_ge(summed, u + 1)
                nc.scalar.activation(mean, rowsum[:, u:u + 1], ACT.Copy, scale=-1.0 / D).then_inc(mean_done, 1)
                act.wait_ge(mean_done, u + 1)
                nc.scalar.activation(tile[u % 2], tile[u % 2], ACT.Identity, bias=mean).then_inc(centred, 1)
                act.wait_ge(centred, u + 1)
                nc.scalar.activation(stage_h[:, st, k, :], tile[u % 2], ACT.Copy,
                                     scale=1.0 if gain is None else gain).then_inc(stage_hi, 1)

            def path_tile(l, k):
                act.wait_ge(scaled, l * KT + k + 1)
                stage_sum(PATH_U[l] + k, tile[k % 2])
                stage_high(PATH_U[l] + k, 2 * l + 1, k)

            def ent_sum(l, k):
                if k == 0:
                    act.wait_ge(step_done, (l + 1) * FT)
                act.wait_ge(stage_done, ENT_U[l] + k - 1)
                stage_sum(ENT_U[l] + k, bank[KT + k][:, :])

            def ent_tile_high(l, k):
                stage_high(ENT_U[l] + k, 2 * l, k)

            def stack_a(bb, source):
                act.wait_ge(a_mm, bb + 1)
                for rows in STACK:
                    nc.scalar.activation(a_stack[rows, :], source[STACK[0], :], ACT.Copy).then_inc(a_stacked, 1)

            def lora_high(bb, c, place):
                act.wait_ge(lsum_done, bb * ITEMS + c)
                k, q = lora_tile(c)
                nc.scalar.activation(mb_h[:, k, q], place[c % 2], ACT.Copy).then_inc(lhi, 1)

            def x_high(bb, k):
                act.wait_ge(x_in, bb * 16 + 16)
                nc.scalar.activation(x_h[:, k, :], amp[:, k, :], ACT.Copy).then_inc(xhi, 1)

            def gate(bb, s, place):
                m = s % KT
                act.wait_ge(s_mm, bb * NSLICE + s + 1)
                if s < KT:
                    nc.scalar.activation(place[m], bank[m][:, :], ACT.Tanh,
                                         bias=col[:, PH_B + m:PH_B + m + 1]).then_inc(s_act, 1)
                else:
                    nc.scalar.activation(place[m], bank[m][:, :], ACT.Sigmoid,
                                         bias=col[:, AMP_B + m:AMP_B + m + 1]).then_inc(s_act, 1)

            def turn_abs(bb, m, place):
                act.wait_ge(s_act, bb * NSLICE + m + 1)
                nc.scalar.activation(place[m], place[m], ACT.Abs,
                                     bias=minus_quarter[:, :]).then_inc(abs_done, 1)

            def turn_sin(bb, m, place):
                act.wait_ge(abs_done, bb * KT + m + 1)
                nc.scalar.activation(place[m], place[m], ACT.Sin, scale=-math.pi,
                                     bias=half_pi[:, :]).then_inc(sin_done, 1)

            def h_high(bb, m, place):
                act.wait_ge(h_done, bb * KT + m + 1)
                nc.scalar.activation(h_h[:, m, :], place[m], ACT.Copy).then_inc(hhi, 1)

            for k in range(RING):
                ent_split(0, k)
            for m in range(KT):
                act.wait_ge(m_mm, m + 1)
                nc.scalar.activation(fold[:, m, 0:D], bank[m][:, :], ACT.Copy).then_inc(m_act, 1)
            for h in range(2):
                act.wait_ge(q_mm, h + 1)
                nc.scalar.activation(q_h[:, h * D:(h + 1) * D], bank[h][:, :], ACT.Copy).then_inc(q_hi, 1)
            act.wait_ge(scaled_a, 1)
            nc.scalar.activation(am_h[:, :], a_raw, ACT.Copy).then_inc(a_split, 1)
            act.wait_ge(mod_mm, 1)
            for p in range(2):
                nc.scalar.activation(mod[:, p, :], bank[2 + p][:, :], ACT.Copy).then_inc(mod_in, 1)
            stack_a(0, bank[0])

            def ent_and_path(l, k):
                ent_split(l, k)
                if k in PATH_TILE[l]:
                    path_tile(l, PATH_TILE[l].index(k))

            for j in range(RING):
                for c in LORA_EARLY.get(j, ()):
                    lora_high(0, c, lsum_first)
                ent_and_path(0, RING + j)

            for k in range(2 * RING, FT):
                ent_and_path(0, k)
                for c in LORA_LATE.get(k - 2, ()):
                    lora_high(0, c, gates)
                if k in X_FIRST:
                    x_high(0, X_FIRST.index(k))
            act.wait_ge(mod_mm, 2)
            for p in range(2):
                nc.scalar.activation(mod[:, p, :], bank[2 + p][:, :], ACT.Copy).then_inc(mod_in, 1)
            ent_split(1, 0)
            ent_sum(0, 0)
            ent_sum(0, 1)
            ent_tile_high(0, 0)
            ent_tile_high(0, 1)
            ent_sum(0, 2)
            ent_tile_high(0, 2)
            ent_sum(0, 3)
            ent_tile_high(0, 3)
            act.wait_ge(llo, ITEMS)
            ent_split(1, 1)
            ent_split(1, 2)
            gate(0, 0, gates)
            gate(0, 1, gates)
            ent_and_path(1, 3)
            gate(0, 2, gates)
            gate(0, 3, gates)
            for k in range(RING, FT):
                ent_and_path(1, k)
                if k < 2 * RING:
                    turn_abs(0, k - RING, gates)
                elif k < 3 * RING:
                    turn_sin(0, k - 2 * RING, gates)
                elif k == 3 * RING:
                    nc.scalar.activation(unread[:, :], half_pi[:, :], ACT.Sigmoid)

            def bias_row_sum(n):
                st = BIAS_ORDER[n]
                act.wait_ge(bias_mm, n + 1)
                nc.scalar.activation(bias[:, st, :], bank[KT + st][:, :], ACT.Copy,
                                     accum_out=rowsum[:, 16 + st:17 + st]).then_inc(bias_sum, 1)

            ent_sum(1, 0)
            ent_sum(1, 1)
            ent_tile_high(1, 0)
            ent_tile_high(1, 1)
            gate(0, KT, turn)
            ent_sum(1, 2)
            ent_tile_high(1, 2)
            h_high(0, 0, gates)
            gate(0, KT + 1, turn)
            ent_sum(1, 3)
            ent_tile_high(1, 3)
            h_high(0, 1, gates)
            act.wait_ge(acc_done, L * FT)
            gate(0, KT + 2, turn)
            gate(0, KT + 3, turn)
            h_high(0, 2, gates)
            h_high(0, 3, gates)
            for n in range(STAGES):
                bias_row_sum(n)

            def z_high(b, st, i):
                t = st * NT + i
                act.wait_ge(t_mm, b * 12 + t + 1)
                nc.scalar.activation(z_h[:, :, i * P:(i + 1) * P],
                                     bank[4 + t % 2][:, :].rearrange("p (k t) -> p k t", k=KT),
                                     ACT.Copy).then_inc(zhi, 1)

            def square(b, st, i):
                n = st * NT + i
                if n:
                    act.wait_ge(sq_done, b * 16 + n)
                act.wait_ge(v_done, b * 16 + n + 1 + NT)
                nc.scalar.activation(bank[7][:, :], work[:, i, :], ACT.Square,
                                     accum_out=sumsq[:, n:n + 1]).then_inc(sq_done, 1)

            def batch(b, with_next):
                if with_next:
                    act.wait_ge(hlo, b * KT + KT)
                    act.dma_start(amp[:, :, :], xt[bass.ds(b + 1, 1)].rearrange(
                        "a p k t -> (a p) k t")).then_inc(x_in, 16)
                seq = order(with_next)
                for pos, (kind, one, two) in enumerate(seq):
                    if pos >= LAG and transposed(seq[pos - LAG]):
                        z_high(b, *seq[pos - LAG][1:])
                    if kind == "Y":
                        square(b, one, two)
                    else:
                        if one == 2:
                            act.wait_ge(llo, (b + 1) * ITEMS + ITEMS)
                        gate(b + 1, one, turn if one < KT else gates)
                        if 0 < one < KT:
                            turn_abs(b + 1, one - 1, turn)
                        if one > KT:
                            h_high(b + 1, one - KT - 1, turn)
                        if one == KT - 1:
                            turn_abs(b + 1, KT - 1, turn)
                            for m in range(KT):
                                turn_sin(b + 1, m, turn)
                        if one == NSLICE - 1:
                            h_high(b + 1, KT - 1, turn)
                    if with_next:
                        if pos == SELECT_AT:
                            stack_a(b + 1, bank[6])
                        if LORA_AT <= pos < LORA_AT + NSLICE:
                            lora_high(b + 1, pos - LORA_AT + 1, lsum)
                        if pos in X_AT:
                            x_high(b + 1, pos - X_AT[0])

            with act.Fori(0, B - 1) as b:
                batch(b, True)
            batch(B - 1, False)

        @block.vector
        def _(dve):
            own = Tally(dve_chain)
            ph, kk = gb[0:4, 0, :], work[0:4, 0, :]

            def fold_low(k):
                dve.wait_ge(hi_done, 3 * k + 1)
                nc.vector.tensor_tensor(x_l[:, k, :], amp[:, k, :], x_h[:, k, :].bitcast(F32),
                                        ALU.subtract).then_inc(lo_done, 1)
                for n, c in enumerate((slice(0, D), slice(D, 2 * D))):
                    dve.wait_ge(hi_done, 3 * k + n + 2)
                    nc.vector.tensor_tensor(mb_l[:, k, c], fold[:, k, c], mb_h[:, k, c].bitcast(F32),
                                            ALU.subtract).then_inc(lo_done, 1)

            for k in range(KT):
                fold_low(k)
            dve.wait_ge(b_hi, 1)
            nc.vector.tensor_tensor(am_l[:, :], b_raw, am_h[:, :].bitcast(F32), ALU.subtract).then_inc(b_lo, 1)

            dve.wait_ge(rows_in, 32)
            own.inc(nc.vector.tensor_scalar(kk, ph, 1.0 / (2 * math.pi), ROUND, ALU.mult, ALU.add), dve)
            own.inc(nc.vector.tensor_scalar(kk, kk, ROUND, None, ALU.subtract), dve)
            for part in TWO_PI:
                own.inc(nc.vector.scalar_tensor_tensor(ph, kk, -part, ph, ALU.mult, ALU.add), dve)
            nc.vector.tensor_scalar(ph, ph, PI_BELOW, -PI_BELOW, ALU.min, ALU.max).then_inc(reduced, 1)

            dve.wait_ge(trig, 2)
            dve.wait_ge(const_done, 5)
            nc.vector.tensor_tensor(mod_rows, work[0:4, 1, :], work[0:4, 0, :], ALU.add).then_inc(rows_done, 1)
            for l in range(L):
                own.inc(nc.vector.tensor_tensor(layer_rows[:, l:l + 1], ident[:, 2 * l:2 * l + 1],
                                                ident[:, 2 * l + 1:2 * l + 2], ALU.add), dve)
            dve.wait_ge(rows_done, 1)
            for l in range(L):
                nc.vector.scalar_tensor_tensor(bias[0:4, 2 * l + 1, :], gb[0:4, 1, :], layer_rows[0:4, l:l + 1],
                                               mod_rows, ALU.mult, ALU.mult).then_inc(rows_done, 1)

            dve.wait_ge(const_done, 5)
            for unit in (2, 4, 5):
                nc.vector.tensor_copy(target[:, unit * RANK:(unit + 1) * RANK], target_i[:, :])
            dve.wait_ge(small_in, 32)
            own.inc(nc.vector.tensor_copy(idx_f[:, :], idx_i[:, :]), dve)
            own.inc(nc.vector.tensor_scalar(idx_f[:, :], idx_f[:, :], float(RANK), None, ALU.mult), dve)
            dve.wait_ge(a_in, 16)
            nc.vector.tensor_scalar(a_raw, a_raw, col[:, SCALE:SCALE + 1], None, ALU.mult).then_inc(scaled_a, 1)

            def select_rows(bb):
                nc.vector.tensor_scalar(select[:, :], target[:, :], idx_f[:, bass.ds(bb, 1)], None,
                                        ALU.is_equal).then_inc(select_done, 1)

            def stack_q(bb, half, source):
                dve.wait_ge(q_sel_mm, 2 * bb + half + 1)
                nc.vector.tensor_copy(q_stack[STACK[half], :], source[STACK[0], :]).then_inc(q_stacked, 1)

            def ent_low(l, k):
                raw2 = raw_slot[at["E", l, k] % RING].rearrange("p (a b) -> p a b", a=2)
                slot, e = k % RING, l * FT + k
                dve.wait_ge(hi_done, LO_FOLD + e + 1)
                nc.vector.tensor_tensor(ring_l[slot], raw2, ring_h[slot].bitcast(F32),
                                        ALU.subtract).then_inc(lo_done, 1)
                if e == 0:
                    dve.wait_ge(entpb_in, 32)
                else:
                    dve.wait_ge(acc_done, e)
                nc.vector.scalar_tensor_tensor(bias[:, 2 * l, :], raw2[:, 1, :], col[:, ENT_B + e:ENT_B + e + 1],
                                               bias[:, 2 * l, :], ALU.mult, ALU.add).then_inc(acc_done, 1)

            def stage_tile(u, st, k):
                t = tile[u % 2]
                gain, shift = gain_col(st, k), shift_col(st, k)
                if shift is not None:
                    dve.wait_ge(centred, u + 1)
                    if st % 2 == 0:
                        dve.wait_ge(acc_done, (st // 2 + 1) * FT)
                    own.inc(nc.vector.scalar_tensor_tensor(bias[:, st, :], t, shift, bias[:, st, :],
                                                           ALU.mult, ALU.add), dve)
                dve.wait_ge(stage_hi, u + 1)
                high = stage_h[:, st, k, :].bitcast(F32)
                if gain is None:
                    low = nc.vector.tensor_tensor(stage_l[:, st, k, :], t, high, ALU.subtract)
                else:
                    low = nc.vector.scalar_tensor_tensor(stage_l[:, st, k, :], t, gain, high,
                                                         ALU.mult, ALU.subtract)
                low.then_inc(stage_done, 1)

            def ent_and_path(l, k):
                ent_low(l, k)
                if k in PATH_TILE[l]:
                    path = PATH_TILE[l].index(k)
                    stage_tile(PATH_U[l] + path, 2 * l + 1, path)

            def lora_sum(bb, c, place, source):
                k, q = lora_tile(c)
                if c > 2:
                    dve.wait_ge(llo, bb * ITEMS + c - 2)
                dve.wait_ge(l_mm, bb * NSLICE + c)
                nc.vector.tensor_tensor(place[c % 2], source, fold[:, k, q], ALU.add).then_inc(lsum_done, 1)

            def lora_low(bb, c, place):
                k, q = lora_tile(c)
                dve.wait_ge(lhi, bb * ITEMS + c)
                nc.vector.tensor_tensor(mb_l[:, k, q], place[c % 2], mb_h[:, k, q].bitcast(F32),
                                        ALU.subtract).then_inc(llo, 1)

            def x_low(bb, k):
                dve.wait_ge(xhi, bb * KT + k + 1)
                nc.vector.tensor_tensor(x_l[:, k, :], amp[:, k, :], x_h[:, k, :].bitcast(F32),
                                        ALU.subtract).then_inc(xlo, 1)

            for k in range(RING):
                ent_low(0, k)
            for m in range(KT):
                dve.wait_ge(m_mm, KT + m + 1)
                nc.vector.tensor_copy(fold[:, m, D:2 * D], bank[KT + m][:, :]).then_inc(m_dve, 1)
            select_rows(0)
            for h in range(2):
                dve.wait_ge(q_hi, h + 1)
                nc.vector.tensor_tensor(q_l[:, h * D:(h + 1) * D], bank[h][:, :],
                                        q_h[:, h * D:(h + 1) * D].bitcast(F32), ALU.subtract).then_inc(q_lo, 1)
            dve.wait_ge(a_split, 1)
            nc.vector.tensor_tensor(am_l[:, :], a_raw, am_h[:, :].bitcast(F32), ALU.subtract).then_inc(a_split, 1)
            dve.wait_ge(m_act, KT)
            for j in range(RING):
                if j == 0:
                    stack_q(0, 0, bank[1])
                    stack_q(0, 1, bank[2])
                early = LORA_EARLY.get(j, ())
                for c in early:
                    lora_sum(0, c, lsum_first, bank[first_bank(c)][:, :])
                for c in early:
                    lora_low(0, c, lsum_first)
                ent_and_path(0, RING + j)
            def ent_tile(l, k):
                stage_tile(ENT_U[l] + k, 2 * l, k)

            def h_product(bb, m, place, gate):
                dve.wait_ge(sin_done, bb * KT + m + 1)
                dve.wait_ge(s_act, bb * NSLICE + KT + m + 1)
                nc.vector.scalar_tensor_tensor(place[m], place[m], math.sqrt(2), gate[m],
                                               ALU.mult, ALU.mult).then_inc(h_done, 1)

            def h_low(bb, m, place):
                dve.wait_ge(hhi, bb * KT + m + 1)
                nc.vector.tensor_tensor(h_l[:, m, :], place[m], h_h[:, m, :].bitcast(F32),
                                        ALU.subtract).then_inc(hlo, 1)

            for k in range(2 * RING, FT):
                ent_and_path(0, k)
                late = LORA_LATE.get(k - 2, ())
                if 5 in late:
                    dve.wait_ge(xlo, KT)
                for c in late:
                    lora_sum(0, c, gates, bank[first_bank(c)][:, :])
                for c in late:
                    lora_low(0, c, gates)
                if k in X_FIRST:
                    x_low(0, X_FIRST.index(k))
            ent_low(1, 0)
            ent_tile(0, 0)
            ent_tile(0, 1)
            ent_tile(0, 2)
            ent_tile(0, 3)
            ent_low(1, 1)
            for k in range(2, FT):
                ent_and_path(1, k)
            ent_tile(1, 0)
            ent_tile(1, 1)
            h_product(0, 0, gates, turn)
            ent_tile(1, 2)
            h_low(0, 0, gates)
            h_product(0, 1, gates, turn)
            ent_tile(1, 3)
            h_low(0, 1, gates)
            h_product(0, 2, gates, turn)

            def bias_centre(n):
                st = BIAS_ORDER[n]
                c = slice(16 + st, 17 + st)
                dve.wait_ge(bias_sum, n + 1)
                own.inc(nc.vector.tensor_scalar(negmean[:, c], rowsum[:, c], -1.0 / D, None, ALU.mult), dve)
                nc.vector.tensor_scalar(bias[:, st, :], bias[:, st, :], negmean[:, c], None,
                                        ALU.add).then_inc(bias_done, 1)

            h_product(0, 3, gates, turn)
            h_low(0, 2, gates)
            h_low(0, 3, gates)
            for n in range(STAGES):
                bias_centre(n)
            dve.wait_ge(bias_done, STAGES)

            def stage_out(b, st, i):
                n = st * NT + i
                dve.wait_ge(y_mm, b * 16 + n + 1)
                if st == 0:
                    dve.wait_ge(out_done, b * NT + i + 1)
                    nc.vector.tensor_tensor(work[:, i, :], bank[i][:, :], bias[:, st, :],
                                            ALU.add).then_inc(v_done, 1)
                else:
                    dve.wait_ge(r_done, b * 8 + (n - NT) // 2 + 1)
                    nc.vector.scalar_tensor_tensor(work[:, i, :], bank[i][:, :], rstd[:, n - NT:n - NT + 1],
                                                   bias[:, st, :], ALU.mult, ALU.add).then_inc(v_done, 1)

            def z_low(b, st, i):
                t = st * NT + i
                dve.wait_ge(zhi, b * 12 + t + 1)
                nc.vector.tensor_tensor(z_l[:, :, i * P:(i + 1) * P],
                                        bank[4 + t % 2][:, :].rearrange("p (k t) -> p k t", k=KT),
                                        z_h[:, :, i * P:(i + 1) * P].bitcast(F32), ALU.subtract).then_inc(zlo, 1)

            def gain_out(b, i):
                n = (STAGES - 1) * NT + i
                dve.wait_ge(r_done, b * 8 + n // 2 + 1)
                nc.vector.scalar_tensor_tensor(work[:, i, :], work[:, i, :], rstd[:, n:n + 1], gb[:, 0, :],
                                               ALU.mult, ALU.mult).then_inc(gained, 1)

            def gain_last(b, i):
                dve.wait_ge(v_done, b * 16 + (STAGES - 1) * NT + i + 1 + NT)
                nc.vector.tensor_tensor(turn[i], work[:, i, :], gb[:, 0, :], ALU.mult).then_inc(gained, 1)

            def finish_last(b, i):
                n = (STAGES - 1) * NT + i
                dve.wait_ge(gained, b * NT + i + 1)
                dve.wait_ge(res_done, b * NT + i + 1)
                dve.wait_ge(r_done, b * 8 + n // 2 + 1 + (i == NT - 1))
                nc.vector.scalar_tensor_tensor(res[:, i, :], turn[i], rstd[:, n:n + 1], res[:, i, :],
                                               ALU.mult, ALU.add).then_inc(out_done, 1)

            def batch(b, with_next):
                seq = order(with_next)
                for pos, (kind, one, two) in enumerate(seq):
                    if kind == "Y":
                        stage_out(b, one, two)
                        if not with_next and one == STAGES - 1:
                            gain_last(b, two)
                            if two >= 2:
                                finish_last(b, two - 2)
                    elif one >= KT:
                        h_product(b + 1, one - KT, turn, gates)
                        if one > KT:
                            h_low(b + 1, one - KT - 1, turn)
                        if one == NSLICE - 1:
                            h_low(b + 1, KT - 1, turn)
                    if pos >= LAG and transposed(seq[pos - LAG]):
                        z_low(b, *seq[pos - LAG][1:])
                    if with_next:
                        if pos == 0:
                            select_rows(b + 1)
                        if SELECT_AT < pos < LORA_AT:
                            stack_q(b + 1, pos - SELECT_AT - 1, bank[6])
                        if LORA_AT <= pos < LORA_AT + NSLICE:
                            c = pos - LORA_AT + 1
                            lora_sum(b + 1, c, lsum, bank[6][:, :])
                        if LORA_AT < pos <= LORA_AT + NSLICE:
                            lora_low(b + 1, pos - LORA_AT, lsum)
                        if pos in X_AT:
                            x_low(b + 1, pos - X_AT[0])
                if with_next:
                    for i in range(NT):
                        gain_out(b, i)
                else:
                    finish_last(b, 2)
                    finish_last(b, 3)

            with dve.Fori(0, B - 1) as b:
                batch(b, True)
            batch(B - 1, False)

        @block.tensor
        def _(pe):
            def split_product(dst, parts):
                passes = [(a, b) for lh, ll, rh, rl in parts for a, b in ((lh, rh), (lh, rl), (ll, rh))]
                for n, (a, b) in enumerate(passes):
                    last = nc.tensor.matmul(dst, a, b, start=n == 0, stop=n == len(passes) - 1)
                return last

            def fold_step(slot_h, slot_l, rhs_h, rhs_l, first_bank, first, final, each=None, identity=False):
                for m in range(KT):
                    s = slice(m * P, (m + 1) * P)
                    if identity:
                        nc.tensor.matmul(bank[first_bank + m][:, s], ident[:, :], ident[:, :], start=False,
                                         stop=False)
                    passes = ((slot_h[:, s], rhs_h), (slot_h[:, s], rhs_l), (slot_l[:, s], rhs_h))
                    for n, (a, b) in enumerate(passes):
                        last = nc.tensor.matmul(bank[first_bank + m][:, :], a, b, start=first and n == 0,
                                                stop=final and n == 2)
                    if each is not None and final:
                        last.then_inc(each, 1)
                return last

            pe.wait_ge(const_done, 1)
            for n in range(WARM):
                nc.tensor.matmul(bank[0][:, 0:P], ident[:, :], ident[:, :], start=n == 0, stop=n == WARM - 1)

            for k in range(KT):
                for h in range(2):
                    c = slice(h * D, (h + 1) * D)
                    pe.wait_ge(lo_done, 3 * k + h + 2)
                    fold_step(x_h[:, k, :], x_l[:, k, :], mb_h[:, k, c], mb_l[:, k, c], h * KT,
                              k == 0, k == KT - 1, m_mm)
            pe.wait_ge(b_lo, 1)
            for h in range(2):
                pe.wait_ge(m_act, h + 1)
                c = slice(h * D, (h + 1) * D)
                split_product(bank[h][:, :], [
                    (am_h[:, k * P:(k + 1) * P], am_l[:, k * P:(k + 1) * P], mb_h[:, k, c], mb_l[:, k, c])
                    for k in range(KT)]).then_inc(q_mm, 1)

            def spread_mod(l, first_bank):
                for p in range(2):
                    row = 2 * l + p
                    last = nc.tensor.matmul(bank[first_bank + p][:, :], ident[0:4, row:row + 1].to_broadcast([4, P]),
                                            mod_rows, start=True, stop=True)
                last.then_inc(mod_mm, 1)

            def ent_step(l, j, value, first, final):
                pe.wait_ge(lo_done, LO_FOLD + value)
                fold_step(ring_h[j][:, 0, :], ring_l[j][:, 0, :], ring_h[j][:, 1, :], ring_l[j][:, 1, :],
                          KT, first, final, identity=final).then_inc(step_done, 1)

            def ent_rest(l):
                with pe.Fori(0, FT // RING - 2) as i:
                    for j in range(RING):
                        ent_step(l, j, l * FT + RING + j + 1 + i * RING, False, False)

            def ent_last(l):
                for j in range(RING):
                    ent_step(l, j, (l + 1) * FT - RING + j + 1, False, j == RING - 1)
                    for c in LORA_LATE.get(FT - RING + j, ()) if l == 0 else ():
                        if c > 6:
                            pe.wait_ge(lsum_done, c - 2)
                        lora_product(0, c, bank[first_bank(c)][:, :])

            def select_a(bb, dst):
                pe.wait_ge(select_done, bb + 1)
                nc.tensor.matmul(dst[STACK[0], :], pick_a_high, am_h[:, :], start=True, stop=False)
                nc.tensor.matmul(dst[STACK[0], :], pick_a_low, am_l[:, :], start=False,
                                 stop=True).then_inc(a_mm, 1)

            def select_q(bb, half, dst):
                c = slice((1 - half) * D, (2 - half) * D)
                nc.tensor.matmul(dst[STACK[0], :], pick_q_high, q_h[:, c], start=True, stop=False)
                nc.tensor.matmul(dst[STACK[0], :], pick_q_low, q_l[:, c], start=False,
                                 stop=True).then_inc(q_sel_mm, 1)

            def lora_product(bb, c, dst):
                k, _ = lora_tile(c)
                rows = stack_rows(c)
                if c == 1:
                    pe.wait_ge(a_stacked, 2 * bb + 2)
                    pe.wait_ge(q_stacked, 2 * bb + 2)
                nc.tensor.matmul(dst, a_stack[rows, k * P:(k + 1) * P], q_stack[rows, :], start=True,
                                 stop=True).then_inc(l_mm, 1)

            pe.wait_ge(rows_done, 1)
            pe.wait_ge(m_act, KT)
            spread_mod(0, 2)
            pe.wait_ge(m_dve, KT)
            for j in range(RING):
                ent_step(0, j, j + 1, j == 0, False)
                if j == 0:
                    pe.wait_ge(a_split, 2)
                    pe.wait_ge(q_lo, 2)
                    select_a(0, bank[0])
                    select_q(0, 0, bank[1])
                    pe.wait_ge(mod_in, 2)
                    select_q(0, 1, bank[2])
                for c in LORA_EARLY.get(j, ()):
                    lora_product(0, c, bank[first_bank(c)][:, :])
            ent_rest(0)
            pe.wait_ge(lsum_done, KT)
            spread_mod(1, 2)
            ent_last(0)

            def slice_product(bb, s, dst):
                c = slice_columns(s)
                if s == 0:
                    pe.wait_ge(xlo, bb * KT + KT)
                    pe.wait_ge(llo, bb * ITEMS + KT)
                if s == KT:
                    pe.wait_ge(llo, bb * ITEMS + ITEMS)
                split_product(dst, [(mb_h[:, k, c], mb_l[:, k, c], x_h[:, k, :], x_l[:, k, :])
                                    for k in range(KT)]).then_inc(s_mm, 1)

            for s in range(KT):
                if s == 0:
                    pe.wait_ge(lsum_done, ITEMS)
                if s == 2:
                    pe.wait_ge(mod_in, 4)
                slice_product(0, s, bank[s][:, :])
            pe.wait_ge(summed, ENT_U[0] + KT)
            for j in range(RING):
                ent_step(1, j, FT + j + 1, j == 0, False)
            ent_rest(1)
            ent_last(1)

            def spread_bias(n):
                st = BIAS_ORDER[n]
                pe.wait_ge(stage_done, STAGES * KT if st == 2 else ENT_U[1])
                nc.tensor.matmul(bank[KT + st][:, :], ones, bias[:, st, :], start=True,
                                 stop=True).then_inc(bias_mm, 1)

            for m in range(KT):
                pe.wait_ge(s_act, m + 1)
                slice_product(0, KT + m, bank[m][:, :])
            pe.wait_ge(summed, ENT_U[1] + KT)
            pe.wait_ge(ones_done, 1)
            for n in range(STAGES):
                spread_bias(n)

            def stage_product(b, st, i, with_next):
                n = st * NT + i
                s = slice(i * P, (i + 1) * P)
                if st == 0:
                    if i == 0:
                        pe.wait_ge(s_act, b * NSLICE + NSLICE)
                        pe.wait_ge(hlo, b * KT + KT)
                    src_h, src_l = h_h, h_l
                else:
                    pe.wait_ge(zlo, b * 12 + n - NT + 1)
                    src_h, src_l = z_h, z_l
                pe.wait_ge(v_done, b * 16 + n + 1)
                if st == STAGES - 1 and with_next:
                    pe.wait_ge(s_act, b * NSLICE + NSLICE + KT + i + 1)
                split_product(bank[i][:, :], [(src_h[:, k, s], src_l[:, k, s], stage_h[:, st, k, :],
                                               stage_l[:, st, k, :]) for k in range(KT)]).then_inc(y_mm, 1)

            def transpose_tile(b, st, i):
                t = st * NT + i
                pe.wait_ge(v_done, b * 16 + t + 1 + NT)
                if t >= 2:
                    pe.wait_ge(zlo, b * 12 + t - 1)
                for k in range(KT):
                    last = nc.tensor.transpose(bank[4 + t % 2][:, k * P:(k + 1) * P], work[:, i, k * P:(k + 1) * P],
                                               ident[:, :])
                last.then_inc(t_mm, 1)

            def batch(b, with_next):
                seq = order(with_next)
                for pos, (kind, one, two) in enumerate(seq):
                    if kind == "Y":
                        stage_product(b, one, two, with_next)
                    else:
                        if one < KT:
                            pe.wait_ge(v_done, b * 16 + 2 * NT + one + 1 + NT)
                        else:
                            pe.wait_ge(s_act, b * NSLICE + NSLICE + one - KT + 1)
                        slice_product(b + 1, one, bank[one % KT][:, :])
                    if pos >= LAG and transposed(seq[pos - LAG]):
                        transpose_tile(b, *seq[pos - LAG][1:])
                    if with_next and pos == SELECT_AT:
                        select_a(b + 1, bank[6])
                    if with_next and SELECT_AT < pos < LORA_AT:
                        half = pos - SELECT_AT - 1
                        if half == 0:
                            pe.wait_ge(a_stacked, 2 * (b + 1) + 2)
                        else:
                            pe.wait_ge(q_stacked, 2 * (b + 1) + 1)
                        select_q(b + 1, half, bank[6])
                    if with_next and LORA_AT <= pos < LORA_AT + NSLICE:
                        c = pos - LORA_AT + 1
                        if c > 1:
                            pe.wait_ge(lsum_done, (b + 1) * ITEMS + c - 1)
                        lora_product(b + 1, c, bank[6][:, :])

            with pe.Fori(0, B - 1) as b:
                batch(b, True)
            batch(B - 1, False)


def kernel(**inputs):
    import numpy as np
    import concourse.bacc as bacc
    from concourse.bass_utils import run_bass_kernel_spmd

    def a(name):
        return np.asarray(inputs[name])

    def columns(v, tiles):
        return v.reshape(-1, tiles, P).transpose(2, 0, 1).reshape(P, -1)

    f = lambda name: a("L0_ffn_" + name)
    x = a("x")
    tokens = x.reshape(B, P, NT, D)
    arrays = {
        "xt": tokens.reshape(B, P, NT, KT, P).transpose(0, 4, 3, 2, 1).reshape(B, P, KT, T),
        "xr": tokens,
        "wc": a("L0_cond_W").reshape(KT, P, D),
        "ap": np.concatenate([f("amp_w"), f("ph_w")], axis=1).reshape(KT, P, 2 * D),
        "bt": a("L0_cond_Bm").reshape(NADAPT, KT, P, RANK).transpose(2, 1, 0, 3).reshape(P, KT * NADAPT * RANK),
        "aa": a("L0_cond_A").reshape(NADAPT * RANK, D),
        "idx": a("itok_B_0_6"),
        "cols": np.concatenate([
            columns(f("amp_b"), KT), columns(f("ph_b"), KT), columns(f("ent_b"), FT),
            columns(f("ln3_g"), KT), columns(f("ln3_b"), KT), columns(f("ln4_g"), KT), columns(f("ln4_b"), KT),
            np.repeat(a("L0_cond_scalings"), RANK).reshape(P, 1)], axis=1),
        "phase": f("phase").reshape(L * 2, D),
        "pathb": f("path_b").reshape(L * 2, D),
        "entpb": f("ent_pb"),
        "gb_rows": np.stack([f("ln4_g")[L - 1], f("ln4_b")[L - 1]]),
        "ent": np.concatenate([f("ent_w").transpose(0, 2, 1), f("ent_pw")], axis=2).reshape(L, FT, P, 2 * D),
        "path": f("path_w").reshape(L, 2, KT, P, D).transpose(0, 2, 3, 1, 4).reshape(L, KT, P, 2 * D),
    }
    nc = bacc.Bacc("TRN2", target_bir_lowering=False, num_devices=1, dynamic_dma_scratch_size=1024)
    sent, args = {}, []
    for name, v in arrays.items():
        v = np.ascontiguousarray(v)
        sent["in_" + name] = v
        args.append(nc.dram_tensor("in_" + name, v.shape, mybir.dt.from_np(v.dtype), kind="ExternalInput").ap())
    out = nc.dram_tensor("out_0", (B, P, NT, D), F32, kind="ExternalOutput").ap()
    build(nc, *args, out)
    r = run_bass_kernel_spmd(nc, [sent], core_ids=[0])
    return r.results[0]["out_0"].reshape(B, T, D)
```
